# Optimizing a Trainium2 kernel written in Bass

```python
import numpy as np
import jax
import jax.numpy as jnp

def _softmax(x, axis=-1):
    return jax.nn.softmax(x, axis=axis)

def _gelu(x):
    return jax.nn.gelu(x, approximate=True)

def _silu(x):
    return jax.nn.silu(x)

def _sigmoid(x):
    return jax.nn.sigmoid(x)

def _layernorm(x, axis=-1, eps=1e-05):
    m = jnp.mean(x, axis=axis, keepdims=True)
    v = jnp.var(x, axis=axis, keepdims=True)
    return (x - m) / jnp.sqrt(v + eps)

def _scatter_add(tgt, idx, src, axis=0):
    return tgt.at[idx].add(src)

def _segment_sum(src, seg, n):
    return jax.ops.segment_sum(src, seg, n)
kernel_name = 'mk_lm_tower_d1_tok_ids2048_r4_351864'

def setup_inputs(seed: int=0):
    np.random.seed(seed)
    _w = jnp.asarray

    def _rec_inputs():
        import jax
        import jax.numpy as jnp
        _rk = jax.random.key(seed)
        x = jax.random.randint(jax.random.fold_in(_rk, 1), (1, 2048), 0, 128, jnp.int32)
        return x
    x = _rec_inputs()

    def _L0_tok_setup():
        import jax, jax.numpy as jnp
        import numpy as np
        VOCAB = 128
        D_VIS = 512
        D_TXT = 512
        EPS = 1e-06
        VOCAB_OFFSET = 0

        def rms_norm(x, weight, eps):
            xf = x.astype(jnp.float32)
            var = jnp.mean(xf * xf, axis=-1, keepdims=True)
            normed = xf * jax.lax.rsqrt(var + eps)
            if weight is not None:
                normed = normed * weight.astype(jnp.float32)
            return normed.astype(x.dtype)
        key = jax.random.key(seed)
        k_ids, k_emb, k_w, k_proj = jax.random.split(key, 4)
        input_ids = jax.random.randint(k_ids, (8, 1024), 0, VOCAB, dtype=jnp.int64)
        emb_table = jax.random.normal(k_emb, (VOCAB, D_VIS), dtype=jnp.float32) * 0.02
        norm_weight = jnp.ones((D_VIS,), dtype=jnp.float32) + 0.01 * jax.random.normal(k_w, (D_VIS,), dtype=jnp.float32)
        proj_weight = jax.random.normal(k_proj, (D_TXT, D_VIS), dtype=jnp.float32) * 0.02
        return {'input_ids': input_ids, 'emb_table': emb_table, 'norm_weight': norm_weight, 'proj_weight': proj_weight}
    _L0_tok_all = _L0_tok_setup()
    _L0_tok_in = {k: v for k, v in _L0_tok_all.items() if k in ('emb_table', 'norm_weight', 'proj_weight')}
    del _L0_tok_all

    def _L0_attn_setup():
        import jax, jax.numpy as jnp
        import numpy as np
        D_MODEL = 512
        N_HEADS = 16
        HEAD_DIM = D_MODEL // N_HEADS
        B, T = (2, 512)
        key = jax.random.key(seed)
        ks = jax.random.split(key, 9)
        s = 0.02
        x = jax.random.normal(ks[0], (B, T, D_MODEL), dtype=jnp.float32)
        Wq = jax.random.normal(ks[1], (N_HEADS, D_MODEL, HEAD_DIM), dtype=jnp.float32) * s
        bq = jax.random.normal(ks[2], (N_HEADS, HEAD_DIM), dtype=jnp.float32) * s
        Wk = jax.random.normal(ks[3], (N_HEADS, D_MODEL, HEAD_DIM), dtype=jnp.float32) * s
        bk = jax.random.normal(ks[4], (N_HEADS, HEAD_DIM), dtype=jnp.float32) * s
        Wv = jax.random.normal(ks[5], (N_HEADS, D_MODEL, HEAD_DIM), dtype=jnp.float32) * s
        bv = jax.random.normal(ks[6], (N_HEADS, HEAD_DIM), dtype=jnp.float32) * s
        Wo = jax.random.normal(ks[7], (D_MODEL, D_MODEL), dtype=jnp.float32) * s
        bo = jax.random.normal(ks[8], (D_MODEL,), dtype=jnp.float32) * s
        return {'x': x, 'Wq': Wq, 'bq': bq, 'Wk': Wk, 'bk': bk, 'Wv': Wv, 'bv': bv, 'Wo': Wo, 'bo': bo}
    _L0_attn_all = _L0_attn_setup()
    _L0_attn_in = {k: v for k, v in _L0_attn_all.items() if k in ('Wq', 'bq', 'Wk', 'bk', 'Wv', 'bv', 'Wo', 'bo')}
    del _L0_attn_all

    def _L0_ffn_setup():
        import jax, jax.numpy as jnp
        import numpy as np
        HID = 512
        INTER = 2048
        NEXP = 8
        TOPK = 2
        EPS = 1e-05

        def _mock_fused_moe(x, selected_experts, routing_weights, expert_weight):
            y = jnp.einsum('bsh,hd->bsd', x, expert_weight)
            scale = routing_weights.sum(axis=-1, keepdims=True)
            return y * scale
        key = jax.random.key(seed)
        ks = jax.random.split(key, 6)
        s = lambda fan_in: 1.0 / np.sqrt(fan_in)
        return {'hidden_states': jax.random.normal(ks[0], (4, 1024, HID), dtype=jnp.float32), 'gate_w': jax.random.uniform(ks[1], (HID, NEXP), jnp.float32, -s(HID), s(HID)), 'up_w': jax.random.uniform(ks[2], (HID, INTER), jnp.float32, -s(HID), s(HID)), 'down_w': jax.random.uniform(ks[3], (INTER, HID), jnp.float32, -s(INTER), s(INTER)), 'expert_weight': jax.random.normal(ks[4], (HID, HID), dtype=jnp.float32), 'ln_gamma': jnp.ones((HID,), jnp.float32), 'ln_beta': jnp.zeros((HID,), jnp.float32)}
    _L0_ffn_all = _L0_ffn_setup()
    _L0_ffn_in = {k: v for k, v in _L0_ffn_all.items() if k in ('gate_w', 'up_w', 'down_w', 'expert_weight', 'ln_gamma', 'ln_beta')}
    del _L0_ffn_all
    return {'x': x, 'L0_tok_emb_table': _L0_tok_in['emb_table'], 'L0_tok_norm_weight': _L0_tok_in['norm_weight'], 'L0_tok_proj_weight': _L0_tok_in['proj_weight'], 'L0_attn_Wq': _L0_attn_in['Wq'], 'L0_attn_bq': _L0_attn_in['bq'], 'L0_attn_Wk': _L0_attn_in['Wk'], 'L0_attn_bk': _L0_attn_in['bk'], 'L0_attn_Wv': _L0_attn_in['Wv'], 'L0_attn_bv': _L0_attn_in['bv'], 'L0_attn_Wo': _L0_attn_in['Wo'], 'L0_attn_bo': _L0_attn_in['bo'], 'L0_ffn_gate_w': _L0_ffn_in['gate_w'], 'L0_ffn_up_w': _L0_ffn_in['up_w'], 'L0_ffn_down_w': _L0_ffn_in['down_w'], 'L0_ffn_expert_weight': _L0_ffn_in['expert_weight'], 'L0_ffn_ln_gamma': _L0_ffn_in['ln_gamma'], 'L0_ffn_ln_beta': _L0_ffn_in['ln_beta']}

def reference(x, L0_tok_emb_table, L0_tok_norm_weight, L0_tok_proj_weight, L0_attn_Wq, L0_attn_bq, L0_attn_Wk, L0_attn_bk, L0_attn_Wv, L0_attn_bv, L0_attn_Wo, L0_attn_bo, L0_ffn_gate_w, L0_ffn_up_w, L0_ffn_down_w, L0_ffn_expert_weight, L0_ffn_ln_gamma, L0_ffn_ln_beta):
    import jax
    import jax.numpy as jnp

    def _L0_tok_ref(input_ids, emb_table, norm_weight, proj_weight):
        import jax, jax.numpy as jnp
        import numpy as np
        VOCAB = 128
        D_VIS = 512
        D_TXT = 512
        EPS = 1e-06
        VOCAB_OFFSET = 0

        def rms_norm(x, weight, eps):
            xf = x.astype(jnp.float32)
            var = jnp.mean(xf * xf, axis=-1, keepdims=True)
            normed = xf * jax.lax.rsqrt(var + eps)
            if weight is not None:
                normed = normed * weight.astype(jnp.float32)
            return normed.astype(x.dtype)
        hard_emb = emb_table[input_ids - VOCAB_OFFSET]
        hard_emb_norm = rms_norm(hard_emb, norm_weight, EPS)
        proj = jnp.einsum('bsd,ed->bse', hard_emb_norm, proj_weight)
        return rms_norm(proj, None, EPS)

    def _L0_attn_ref(x, Wq, bq, Wk, bk, Wv, bv, Wo, bo):
        import jax, jax.numpy as jnp
        import numpy as np
        D_MODEL = 512
        N_HEADS = 16
        HEAD_DIM = D_MODEL // N_HEADS
        B, T = (2, 512)
        Bn, Tn, C = x.shape
        H, _, D = Wq.shape
        scale = D ** (-0.5)
        q = jnp.einsum('btc,hcd->bhtd', x, Wq) + bq[None, :, None, :]
        k = jnp.einsum('btc,hcd->bhtd', x, Wk) + bk[None, :, None, :]
        v = jnp.einsum('btc,hcd->bhtd', x, Wv) + bv[None, :, None, :]
        scores = jnp.einsum('bhtd,bhsd->bhts', q, k) * scale
        neg = jnp.finfo(scores.dtype).min
        causal = jnp.triu(jnp.full((Tn, Tn), neg, dtype=scores.dtype), k=1)
        probs = jax.nn.softmax(scores + causal, axis=-1)
        y = jnp.einsum('bhts,bhsd->bhtd', probs, v)
        y = y.transpose(0, 2, 1, 3).reshape(Bn, Tn, H * D)
        return y @ Wo + bo

    def _L0_ffn_ref(hidden_states, gate_w, up_w, down_w, expert_weight, ln_gamma, ln_beta):
        import jax, jax.numpy as jnp
        import numpy as np
        HID = 512
        INTER = 2048
        NEXP = 8
        TOPK = 2
        EPS = 1e-05

        def _mock_fused_moe(x, selected_experts, routing_weights, expert_weight):
            y = jnp.einsum('bsh,hd->bsd', x, expert_weight)
            scale = routing_weights.sum(axis=-1, keepdims=True)
            return y * scale
        residuals = hidden_states
        logits = jnp.einsum('bsh,he->bse', hidden_states, gate_w)
        routing_weights, selected_experts = jax.lax.top_k(logits, TOPK)
        h = jnp.einsum('bsh,hi->bsi', residuals, up_w)
        h = jnp.square(jax.nn.relu(h))
        shared_out = jnp.einsum('bsi,ih->bsh', h, down_w)
        moe_out = _mock_fused_moe(hidden_states, selected_experts, routing_weights, expert_weight)
        y = shared_out + moe_out
        mu = y.mean(axis=-1, keepdims=True)
        var = jnp.mean(jnp.square(y - mu), axis=-1, keepdims=True)
        return (y - mu) * jax.lax.rsqrt(var + EPS) * ln_gamma + ln_beta
    h = _L0_tok_ref(x, L0_tok_emb_table, L0_tok_norm_weight, L0_tok_proj_weight)
    h = h + _L0_attn_ref(_layernorm(h, axis=-1), L0_attn_Wq, L0_attn_bq, L0_attn_Wk, L0_attn_bk, L0_attn_Wv, L0_attn_bv, L0_attn_Wo, L0_attn_bo)
    h = h + _L0_ffn_ref(_layernorm(h, axis=-1), L0_ffn_gate_w, L0_ffn_up_w, L0_ffn_down_w, L0_ffn_expert_weight, L0_ffn_ln_gamma, L0_ffn_ln_beta)
    return h

_drawn_inputs = setup_inputs


def setup_inputs(seed=0):
    import zlib

    import numpy as np

    out = dict(_drawn_inputs(seed))
    spreads = {'L0_ffn_ln_gamma': (1.0, 0.2), 'L0_ffn_ln_beta': (0.0, 0.1)}
    factors = {'L0_tok_norm_weight': 24.455,
     'L0_attn_Wq': 8.0,
     'L0_attn_bq': 8.0,
     'L0_attn_Wk': 8.0,
     'L0_attn_bk': 64.0,
     'L0_attn_bv': 5.484,
     'L0_attn_bo': 2.849,
     'L0_ffn_up_w': 4.428,
     'L0_ffn_down_w': 3.903}
    for name, (base, spread) in spreads.items():
        noise = np.random.default_rng([zlib.crc32(name.encode()), seed]).standard_normal(out[name].shape)
        drawn = base * np.exp(spread * noise) if base else spread * noise
        out[name] = jnp.asarray(drawn.astype(out[name].dtype))
    for name, factor in factors.items():
        out[name] = (out[name] * factor).astype(out[name].dtype)
    return out
```

```python
import concourse.bass as bass
from concourse import mybir
from contextlib import ExitStack

F32 = mybir.dt.float32
F16 = mybir.dt.float16
I32 = mybir.dt.int32
ALU = mybir.AluOpType
ACT = mybir.ActivationFunctionType
AX = mybir.AxisListType
ABSMAX = bass.bass_isa.ReduceOp.absmax

P = 128
SEQ = 2048
DM = 512
KC = DM // P
HEADS = 16
HD = DM // HEADS
INTER = 2048
IC = INTER // P
NEXP = 8
GT = 512
GROUPS = SEQ // GT
TILES = GT // P
HQ = HEADS // 4
UNITS = HQ * TILES
RING = 3

EXPERT_BANK = (0, 1, 0, 0)
TOP = 14
XSHIFT = 11
RSHIFT = 17
UNSEEN = 1e30
EPS_RMS = 1e-6
EPS_LN = 1e-5


def tower(nc, ids, ids_col, emb, norm_w, proj_t, wq, wk, wv, bq, bk, bv, wo, bo, up, down, expert, gate, gamma, beta, out):
    ctx = ExitStack()
    with ctx:
        def sb(name, shape, dt):
            return ctx.enter_context(nc.sbuf_tensor(name, shape, dt))

        def sem(name):
            return ctx.enter_context(nc.semaphore(name))

        wo_hl = sb("wo_hl", [P, 2, KC, DM], F16)
        up_hl = sb("up_hl", [P, 2, KC, INTER], F16)
        ex_hl = sb("ex_hl", [P, 2, KC, DM], F16)
        dn_hl = sb("dn_hl", [P, 2, IC, DM], F16)
        gt_hl = sb("gt_hl", [P, 2, KC, NEXP], F16)
        sc_hl = sb("sc_hl", [P, 2, HEADS, P], F16)
        tk_hl = sb("tk_hl", [P, 2, DM], F16)
        oht = sb("oht", [P, SEQ], F16)
        lnc = sb("lnc", [P, SEQ // P, P], F32)
        val = sb("val", [P, DM], F32)
        tadd = sb("tadd", [P, 2, 4, P], F32)
        prob = sb("prob", [P, 2, 4, P], F32)
        probT = sb("probT", [P, 2, 4, GT], F32)
        yt_hl = sb("yt_hl", [P, 2, HQ, GT], F16)
        rawu = sb("rawu", [P, KC * INTER], F32)
        tokr = rawu[:, 0:1024].rearrange("p (b n) -> p b n", b=2)
        xrow = rawu[:, 1024:2048].rearrange("p (b n) -> p b n", b=2)
        h1 = rawu[:, 2048:4096].rearrange("p (j n) -> p j n", j=TILES)
        h1b = rawu[:, 4096:6144].rearrange("p (j n) -> p j n", j=TILES)
        xt_hl = rawu[:, 6144:8192].bitcast(F16).rearrange("p (a k t) -> p a k t", a=2, k=KC)
        rawd = sb("rawd", [P, IC * DM], F32)
        relu = rawd[:, 0:1024].rearrange("p (b n) -> p b n", b=2)
        sqr = rawd[:, 1024:2048].rearrange("p (b n) -> p b n", b=2)
        y = rawd[:, 2048:4096].rearrange("p (j n) -> p j n", j=TILES)
        fin = rawd[:, 4096:5120].rearrange("p (b n) -> p b n", b=2)
        sq_hl = rawd[:, 5120:5120 + RING * DM].bitcast(F16).rearrange("p (b a n) -> p b a n", b=RING, a=2)
        gam = rawd[:, 5120 + RING * DM:5120 + RING * DM + DM]
        bet = rawd[:, 5120 + RING * DM + DM:5120 + RING * DM + 2 * DM]
        raww = yt_hl[:, :, :, :].rearrange("p a k n -> p (a k n)").bitcast(F32).rearrange("p (k n) -> p k n", k=KC)
        rawe = probT[:, 0]
        idf = probT[:, 1].rearrange("p j n -> p (j n)")
        wflat = dn_hl[:, :, :, :].rearrange("p a k n -> p (a k n)").bitcast(F32).rearrange("p (w k n) -> p w k n", w=4, k=KC)
        pj_sb, wq_sb, wk_sb, wv_sb = (wflat[:, i] for i in range(4))
        exf = ex_hl[:, :, :, :].rearrange("p a k n -> p (a k n)")
        ohr = exf[:, 0:2048].rearrange("p (j v) -> p j v", v=P)
        seen = exf[:, 2048:3072].bitcast(F32)
        tflat = tadd[:, :, :, :].rearrange("p b j v -> p (b j v)")
        pflat = prob[:, :, :, :].rearrange("p b j v -> p (b j v)")
        row = tflat[:, 0:DM]
        nrm = tflat[:, DM:2 * DM]
        colT = pflat[:, 0:DM].rearrange("p (k v) -> p k v", k=KC)
        kT = pflat[:, DM:2 * DM].rearrange("p (k v) -> p k v", k=KC)
        tok = sb("tok", [P, DM], F32)
        sflat = sc_hl[:, :, :, :].rearrange("p a h v -> p (a h v)").bitcast(F32)
        bo_sb = sflat[:, 0:DM]
        bv_sb = sflat[:, DM:2 * DM]
        qT = sflat[:, 2 * DM:3 * DM].rearrange("p (k v) -> p k v", k=KC)
        iota_v = sflat[:, 3 * DM:3 * DM + P]
        iota_vi = sflat[:, 3 * DM + P:3 * DM + 2 * P].bitcast(I32)
        ident = sb("ident", [P, P], F32)
        tri = sb("tri", [P, P], F16)
        ones = sb("ones", [P, P], F16)
        iota_p = sb("iota_p", [P, 1], F32)
        iota_pi = sb("iota_pi", [P, 1], I32)
        idc = sb("idc", [P, SEQ // P], F32)
        tmpc2 = sb("tmpc2", [P, SEQ // P], F32)
        tmpc = sb("tmpc", [P, SEQ // P], F32)
        bqk = sb("bqk", [P, 2, KC], F32)
        rawg = sb("rawg", [P, KC, NEXP], F32)
        mxs = sb("mxs", [P, 4], F32)
        mx = sb("mx", [P, 8], F32)
        am = sb("am", [P, 8], F32)
        p2 = sb("p2", [P, 8], F32)
        inv = sb("inv", [P, 8], F32)
        scl = sb("scl", [P, 8], F32)
        kap = sb("kap", [P, 4], F32)
        stat = sb("stat", [P, 2, 8], F32)
        bn0 = sb("bn0", [P, 6], F32)
        carrier = sb("carrier", [P, 1], F32)
        half = sb("half", [P, TILES], F32)
        nmax = sb("nmax", [P, 2, 4], F32)
        rsum = sb("rsum", [P, 2, 4], F32)
        rinv = sb("rinv", [P, 2, 4], F32)
        bnx = sb("bnx", [P, TILES, 6], F32)
        mvx = sb("mvx", [P, TILES, 2], F32)
        vex = sb("vex", [P, TILES], F32)
        rsx = sb("rsx", [P, TILES], F32)
        bny = sb("bny", [P, TILES, 6], F32)
        mvy = sb("mvy", [P, TILES, 2], F32)
        vey = sb("vey", [P, TILES], F32)
        rsy = sb("rsy", [P, TILES], F32)
        top8 = sb("top8", [P, TILES, 8], F32)
        rout = sb("rout", [P, TILES], F32)
        SC, TK, VL, WO, EX, GA, UP, DN = range(8)
        KO, KE, KY = range(3)

        bank = [ctx.enter_context(nc.psum_tensor(f"bank{i}", [P, 512], F32)) for i in range(8)]
        psY, psU, psS, psT = bank[0:4], bank[4:6], bank[6], bank[7]

        ld = {n: sem("ld_" + n) for n in ("idc", "ids", "emb", "nw", "proj", "wq", "wk", "wv", "bqk", "bv", "bo",
                                          "wo", "up", "gate", "ex", "dn", "gam")}
        s_iota, s_pool0, s_dve, s_act = sem("s_iota"), sem("s_pool0"), sem("s_dve"), sem("s_act")
        s_ohr, s_cnt, s_lnraw, s_cmax, s_lnc = sem("s_ohr"), sem("s_cnt"), sem("s_lnraw"), sem("s_cmax"), sem("s_lnc")
        s_var0, s_rs0, s_row, s_rowT, s_colT, s_proj, s_psb = (sem(n) for n in (
            "s_var0", "s_rs0", "s_row", "s_rowT", "s_colT", "s_proj", "s_psb"))
        s_qkv, s_qk, s_tab, s_oht = sem("s_qkv"), sem("s_qk"), sem("s_tab"), sem("s_oht")
        s_mx, s_am, s_scl = sem("s_mx"), sem("s_am"), sem("s_scl")
        s_hi, s_lo, s_val = sem("s_hi"), sem("s_lo"), sem("s_val")
        s_scored, s_added, s_max, s_exp, s_rec, s_norm, s_trn, s_pt = (sem(n) for n in (
            "s_scored", "s_added", "s_max", "s_exp", "s_rec", "s_norm", "s_trn", "s_pt"))
        s_pv, s_yh, s_yl = sem("s_pv"), sem("s_yh"), sem("s_yl")
        s_tg, s_wo, s_tokr, s_h1, s_bn, s_agg, s_ve, s_rs, s_x, s_xt, s_xh, s_xl, s_h1b = (sem(n) for n in (
            "s_tg", "s_wo", "s_tokr", "s_h1", "s_bn", "s_agg", "s_ve", "s_rs", "s_x", "s_xt", "s_xh", "s_xl", "s_h1b"))
        s_gate, s_top, s_rout, s_up, s_relu, s_sq, s_sh, s_sl, s_dn, s_ex, s_moe = (sem(n) for n in (
            "s_gate", "s_top", "s_rout", "s_up", "s_relu", "s_sq", "s_sh", "s_sl", "s_dn", "s_ex", "s_moe"))
        s_yev, s_bny, s_aggy, s_vey, s_rsy, s_z, s_fin = (sem(n) for n in (
            "s_yev", "s_bny", "s_aggy", "s_vey", "s_rsy", "s_z", "s_fin"))
        s_out = [sem("s_out0"), sem("s_out1")]

        def need(eng, s, value):
            if isinstance(value, int) and value <= 0:
                return
            eng.wait_ge(s, value)

        def bc(ap, n, dt_shape):
            return ap.unsqueeze(1).broadcast_to(dt_shape)

        block = ctx.enter_context(nc.Block())

        @block.sync
        def _(sp):
            for b in range(2):
                sp.sem_inc(s_out[b], 16)

            def load(dst, src, name):
                sp.dma_start(dst, src).then_inc(ld[name], 16)

            load(row, emb, "emb")
            load(nrm, norm_w.partition_broadcast(P), "nw")
            load(idc[:, :].bitcast(I32), ids_col, "idc")
            load(pj_sb, proj_t.rearrange("(k p) n -> p k n", p=P), "proj")
            load(idf.bitcast(I32), ids.partition_broadcast(P), "ids")
            load(wq_sb, wq.rearrange("(k p) n -> p k n", p=P), "wq")
            load(wk_sb, wk.rearrange("(k p) n -> p k n", p=P), "wk")
            load(bqk[:, 0], bq, "bqk")
            load(bqk[:, 1], bk, "bqk")
            load(wv_sb, wv.rearrange("(k p) n -> p k n", p=P), "wv")
            load(bv_sb, bv.partition_broadcast(P), "bv")
            load(bo_sb, bo.partition_broadcast(P), "bo")
            load(raww, wo.rearrange("(k p) n -> p k n", p=P), "wo")
            load(rawu[:, :].rearrange("p (k n) -> p k n", k=KC), up.rearrange("(k p) n -> p k n", p=P), "up")
            load(rawe, expert.rearrange("(k p) n -> p k n", p=P), "ex")
            load(rawg[:, :, :], gate.rearrange("(k p) n -> p k n", p=P), "gate")
            load(rawd[:, :].rearrange("p (k n) -> p k n", k=IC), down.rearrange("(k p) n -> p k n", p=P), "dn")
            sp.wait_ge(s_lo, 16)
            load(gam, gamma.partition_broadcast(P), "gam")
            load(bet, beta.partition_broadcast(P), "gam")

            def store(g):
                for j in range(TILES):
                    sp.wait_ge(s_fin, g * TILES + j + 1)
                    sp.dma_start(out[bass.ds(g * GT + j * P, P), :], fin[:, j % 2]).then_inc(s_out[j % 2], 16)

            with sp.Fori(0, GROUPS) as g:
                store(g)
            for b in range(2):
                sp.wait_ge(s_out[b], 16 * (GROUPS * TILES // 2 + 1))

        @block.gpsimd
        def _(pool):
            nc.gpsimd.iota(iota_vi, [[1, P]], base=0, channel_multiplier=0).then_inc(s_iota, 1)
            nc.gpsimd.iota(iota_pi[:, :], [[0, 1]], base=0, channel_multiplier=1).then_inc(s_iota, 1)
            nc.gpsimd.memset(half[:, :], -0.5).then_inc(s_pool0, 1)
            nc.gpsimd.memset(ident[:, :], 0.0).then_inc(s_pool0, 1)
            nc.gpsimd.memset(ones[:, :], 1.0).then_inc(s_pool0, 1)
            pool.wait_ge(s_pool0, 3)
            nc.gpsimd.affine_select(out=ident[:, :], in_=ident[:, :], compare_op=ALU.not_equal, fill=1.0, base=0,
                                    pattern=[[-1, P]], channel_multiplier=1).then_inc(s_pool0, 1)
            nc.gpsimd.affine_select(out=tri[:, :], in_=ones[:, :], compare_op=ALU.is_ge, fill=0.0, base=0,
                                    pattern=[[1, P]], channel_multiplier=-1).then_inc(s_pool0, 1)

            def rsqrt(dst, src, n):
                return nc.gpsimd.tensor_tensor(dst, src, half[:, 0:n], ALU.pow)

            for i in range(3):
                pool.wait_ge(s_var0, i + 1)
                rsqrt(stat[:, 1, i:i + 1], stat[:, 0, i:i + 1], 1).then_inc(s_rs0, 1)
            for i, (a, b) in enumerate(((WO, GA + 1), (SC, VL + 1), (UP, UP + 1), (DN, DN + 1))):
                pool.wait_ge(s_mx, i + 1)
                nc.gpsimd.partition_all_reduce(am[:, a:b], mx[:, a:b], P, ABSMAX).then_inc(s_am, 1)

            def last_norm(g):
                pool.wait_ge(s_vey, g + 1)
                rsqrt(rsy[:, :], vey[:, :], TILES).then_inc(s_rsy, 1)

            for j in range(TILES):
                pool.wait_ge(s_ve, j + 1)
                rsqrt(rsx[:, j:j + 1], vex[:, j:j + 1], 1).then_inc(s_rs, 1)
            for j in range(TILES):
                pool.wait_ge(s_h1, j + 1)
                if j == 0:
                    pool.wait_ge(ld["gam"], 32)
                nc.gpsimd.tensor_tensor(h1b[:, j], h1[:, j], bet, ALU.add).then_inc(s_h1b, 1)
            with pool.Fori(0, GROUPS - 1) as g:
                for j in range(TILES):
                    pool.wait_ge(s_ve, (g + 1) * TILES + j + 1)
                    rsqrt(rsx[:, j:j + 1], vex[:, j:j + 1], 1).then_inc(s_rs, 1)
                last_norm(g)
                for j in range(TILES):
                    pool.wait_ge(s_fin, g * TILES + j + 1)
                    nc.gpsimd.tensor_tensor(h1b[:, j], h1[:, j], bet, ALU.add).then_inc(s_h1b, 1)
            last_norm(GROUPS - 1)

        @block.scalar
        def _(act):
            def copy(dst, src, scale=None):
                if scale is None:
                    return nc.scalar.copy(dst, src)
                return nc.scalar.activation(dst, src, ACT.Copy, scale=scale)

            act.wait_ge(s_rowT, 1)
            copy(colT, psS[:, :]).then_inc(s_colT, 1)
            act.wait_ge(s_proj, 1)
            copy(tok[:, :], psT[:, :]).then_inc(s_psb, 1)
            for b in range(4):
                act.wait_ge(s_cmax, b + 1)
                nc.scalar.activation(lnc[:, 4 * b:4 * b + 4, :], lnc[:, 4 * b:4 * b + 4, :], ACT.Ln).then_inc(s_lnraw, 1)
            act.wait_ge(s_rowT, 2)
            copy(colT, psS[:, :]).then_inc(s_colT, 1)
            act.wait_ge(s_scl, 1)
            copy(wo_hl[:, 0], raww, scl[:, WO:WO + 1]).then_inc(s_hi, 1)
            act.wait_ge(s_lnc, 4)
            copy(ex_hl[:, 0], rawe, scl[:, EX:EX + 1]).then_inc(s_hi, 1)
            copy(gt_hl[:, 0], rawg[:, :, :], scl[:, GA:GA + 1]).then_inc(s_hi, 1)
            act.wait_ge(s_scl, 2)
            for j in range(4):
                copy(sc_hl[:, 0].rearrange("p (c j) v -> p c j v", j=4)[:, :, j, :],
                     bank[j][:, :].rearrange("p (c v) -> p c v", v=P), scl[:, SC:SC + 1]).then_inc(s_hi, 1)
            copy(tk_hl[:, 0], tok[:, :], scl[:, TK:TK + 1]).then_inc(s_hi, 1)

            def exps(u, g):
                act.wait_ge(s_max, g * UNITS + u + 1)
                if u >= 2:
                    act.wait_ge(s_trn, g * UNITS + u - 1)
                for h in range(4):
                    last = nc.scalar.activation(prob[:, u % 2, h, :], tadd[:, u % 2, h, :], ACT.Exp,
                                                bias=nmax[:, u % 2, h:h + 1], accum_out=rsum[:, u % 2, h:h + 1])
                last.then_inc(s_exp, 1)

            def evac_probs(u, g):
                q, j = u // TILES, u % TILES
                act.wait_ge(s_trn, g * UNITS + u + 1)
                if q >= 2 and j == 0:
                    act.wait_ge(s_pv, g * HQ + q - 1)
                copy(probT[:, q % 2, :, j * P:(j + 1) * P],
                     psT[:, :].rearrange("p (h t) -> p h t", h=4)).then_inc(s_pt, 1)

            def evac_y(q, g):
                act.wait_ge(s_pv, g * HQ + q + 1)
                copy(yt_hl[:, 0, q], psT[:, :]).then_inc(s_yh, 1)

            def token_rows(j, g):
                act.wait_ge(s_tg, g * TILES + j + 1)
                if j >= 2:
                    act.wait_ge(s_h1, g * TILES + j - 1)
                copy(tokr[:, j % 2], psS[:, :], inv[:, TK:TK + 1]).then_inc(s_tokr, 1)

            def split_x(j, g, b):
                act.wait_ge(s_xt, g * TILES + j + 1)
                copy(xt_hl[:, 0, :, j * P:(j + 1) * P],
                     psU[b][:, :].rearrange("p (k t) -> p k t", k=KC)).then_inc(s_xh, 1)

            def square(i, g):
                act.wait_ge(s_up, g * IC + i + 1)
                nc.scalar.activation(relu[:, i % 2], psU[i % 2][:, :], ACT.Relu,
                                     scale=2.0 ** -(XSHIFT + RSHIFT)).then_inc(s_relu, 1)
                act.wait_ge(s_relu, g * IC + i + 1)
                if i >= 2:
                    act.wait_ge(s_sl, g * IC + i - 1)
                nc.scalar.activation(sqr[:, i % 2], relu[:, i % 2], ACT.Square).then_inc(s_sq, 1)
                act.wait_ge(s_sq, g * IC + i + 1)
                if i >= RING:
                    act.wait_ge(s_dn, g * IC + i - RING + 1)
                copy(sq_hl[:, i % RING, 0], sqr[:, i % 2]).then_inc(s_sh, 1)

            def attention_alone(g):
                exps(0, g)
                for u in range(UNITS):
                    if u < UNITS - 1:
                        exps(u + 1, g)
                    evac_probs(u, g)
                    if u % TILES == TILES - 1:
                        evac_y(u // TILES, g)

            act.wait_ge(s_lo, 3)
            attention_alone(0)
            act.wait_ge(s_scl, 3)
            for k in range(KC):
                copy(up_hl[:, 0, k], rawu[:, k * INTER:(k + 1) * INTER], scl[:, UP:UP + 1]).then_inc(s_hi, 1)
            act.wait_ge(s_scl, 4)
            for k in range(4):
                copy(dn_hl[:, 0, 4 * k:4 * k + 4], rawd[:, k * 2048:(k + 1) * 2048].rearrange("p (k n) -> p k n", k=4),
                     scl[:, DN:DN + 1]).then_inc(s_hi, 1)
            act.wait_ge(s_lo, 12)
            token_rows(0, 0)
            token_rows(1, 0)
            split_x(0, 0, 1)
            token_rows(2, 0)
            split_x(1, 0, 1)
            token_rows(3, 0)
            split_x(2, 0, 0)
            split_x(3, 0, 1)
            act.wait_ge(s_lo, 16)
            with act.Fori(0, GROUPS - 1) as g:
                for i in range(IC):
                    square(i, g)
                    if i > 0:
                        evac_probs(i - 1, g + 1)
                        if (i - 1) % TILES == TILES - 1:
                            evac_y((i - 1) // TILES, g + 1)
                    exps(i, g + 1)
                evac_probs(UNITS - 1, g + 1)
                evac_y(HQ - 1, g + 1)
                token_rows(0, g + 1)
                token_rows(1, g + 1)
                split_x(0, g + 1, 1)
                token_rows(2, g + 1)
                split_x(1, g + 1, 1)
                token_rows(3, g + 1)
                split_x(2, g + 1, 0)
                split_x(3, g + 1, 1)
            for i in range(IC):
                square(i, GROUPS - 1)

        @block.vector
        def _(dve):
            chain = [0]

            def link(ins):
                chain[0] += 1
                ins.then_inc(s_dve, 1)
                dve.wait_ge(s_dve, chain[0])

            def largest(col, src, ax):
                return nc.vector.tensor_reduce(mx[:, col:col + 1], src, ax, ALU.max, apply_absolute_value=True)

            def wrap(ids_i, f, t):
                link(nc.vector.tensor_scalar(t, ids_i, 0.0, float(P), ALU.is_lt, ALU.mult))
                link(nc.vector.tensor_tensor(f, ids_i, t, ALU.add))
                link(nc.vector.tensor_scalar(f, f, float(P - 1), 0.0, ALU.min, ALU.max))

            def scales(a, b, n):
                dve.wait_ge(s_am, n)
                link(nc.vector.tensor_scalar(p2[:, a:b], am[:, a:b], 2.0 ** -100, 2.0 ** 100, ALU.max, ALU.min))
                link(nc.vector.tensor_scalar(p2[:, a:b].bitcast(I32), p2[:, a:b].bitcast(I32), 0x7F800000, None,
                                             ALU.bitwise_and))
                link(nc.vector.tensor_scalar(inv[:, a:b], p2[:, a:b], 2.0 ** -TOP, None, ALU.mult))
                link(nc.vector.tensor_scalar(scl[:, a:b].bitcast(I32), p2[:, a:b].bitcast(I32), 0x7F800000, None,
                                             ALU.bitwise_xor))
                link(nc.vector.tensor_scalar(scl[:, a:b], scl[:, a:b], 2.0 ** (TOP - 1), None, ALU.mult))
                nc.vector.tensor_scalar(p2[:, a:b], scl[:, a:b], 1.0, None, ALU.mult).then_inc(s_scl, 1)

            lows = [0]

            def low(dst, src, high, col):
                lows[0] += 1
                dve.wait_ge(s_hi, lows[0])
                nc.vector.scalar_tensor_tensor(dst, src, scl[:, col:col + 1], high, ALU.mult,
                                               ALU.subtract).then_inc(s_lo, 1)

            dve.wait_ge(s_iota, 2)
            link(nc.vector.tensor_copy(iota_v, iota_vi))
            link(nc.vector.tensor_copy(iota_p[:, :], iota_pi[:, :]))
            dve.wait_ge(ld["idc"], 16)
            wrap(idc[:, :].bitcast(I32), tmpc2[:, :], tmpc[:, :])
            nc.vector.tensor_tensor(ohr, iota_v.unsqueeze(1).broadcast_to([P, SEQ // P, P]),
                                    tmpc2[:, :].unsqueeze(2).broadcast_to([P, SEQ // P, P]), ALU.is_equal).then_inc(s_ohr, 1)
            dve.wait_ge(ld["emb"], 16)
            link(nc.vector.tensor_tensor_reduce(out=tok[:, :], in0=row, in1=row, scale=1.0, scalar=0.0, op0=ALU.mult,
                                                op1=ALU.add, accum_out=stat[:, 0, 3:4]))
            nc.vector.tensor_scalar(stat[:, 0, 0:1], stat[:, 0, 3:4], 1.0 / DM, EPS_RMS, ALU.mult,
                                    ALU.add).then_inc(s_var0, 1)
            dve.wait_ge(ld["nw"], 16)
            dve.wait_ge(s_rs0, 1)
            nc.vector.scalar_tensor_tensor(row, row, stat[:, 1, 0:1], nrm, ALU.mult, ALU.mult).then_inc(s_row, 1)
            for b in range(4):
                dve.wait_ge(s_cnt, b + 1)
                nc.vector.tensor_scalar(lnc[:, 4 * b:4 * b + 4, :].rearrange("p j v -> p (j v)"), bank[b][:, :], 1.0, None,
                                        ALU.max).then_inc(s_cmax, 1)
            dve.wait_ge(ld["ids"], 16)
            for b in range(4):
                c = slice(b * 512, (b + 1) * 512)
                wrap(idf[:, c].bitcast(I32), idf[:, c], val[:, :])
                last = nc.vector.tensor_scalar(oht[:, c], idf[:, c], iota_p[:, 0:1], None, ALU.is_equal)
                last.then_inc(s_oht, 1)
            dve.wait_ge(s_psb, 1)
            link(nc.vector.tensor_tensor_reduce(out=nrm, in0=tok[:, :], in1=tok[:, :], scale=1.0, scalar=0.0,
                                                op0=ALU.mult, op1=ALU.add, accum_out=stat[:, 0, 3:4]))
            nc.vector.tensor_scalar(stat[:, 0, 1:2], stat[:, 0, 3:4], 1.0 / DM, EPS_RMS, ALU.mult,
                                    ALU.add).then_inc(s_var0, 1)
            dve.wait_ge(s_rs0, 2)
            link(nc.vector.tensor_scalar(tok[:, :], tok[:, :], stat[:, 1, 1:2], None, ALU.mult))
            link(nc.vector.bn_stats(bn0[:, :], tok[:, :]))
            link(nc.vector.bn_aggr(stat[:, 0, 4:6], bn0[:, :]))
            nc.vector.tensor_scalar(stat[:, 0, 2:3], stat[:, 0, 5:6], EPS_LN, None, ALU.add).then_inc(s_var0, 1)
            dve.wait_ge(s_rs0, 3)
            nc.vector.tensor_scalar(row, tok[:, :], stat[:, 0, 4:5], stat[:, 1, 2:3], ALU.subtract,
                                    ALU.mult).then_inc(s_row, 1)
            dve.wait_ge(ld["bo"], 16)
            dve.wait_ge(s_row, 2)
            link(nc.vector.tensor_tensor(tok[:, :], tok[:, :], bo_sb, ALU.add))
            for b in range(4):
                lb = lnc[:, 4 * b:4 * b + 4, :].rearrange("p j v -> p (j v)")
                link(nc.vector.tensor_scalar(seen, bank[b][:, :], 1.0, -1.0, ALU.min, ALU.add))
                dve.wait_ge(s_lnraw, b + 1)
                nc.vector.scalar_tensor_tensor(lb, seen, UNSEEN, lb, ALU.mult, ALU.add).then_inc(s_lnc, 1)
                dve.wait_ge(s_lnc, b + 1)
            dve.wait_ge(ld["wo"], 16)
            link(largest(WO, raww, AX.XY))
            dve.wait_ge(ld["ex"], 16)
            link(largest(EX, rawe, AX.XY))
            dve.wait_ge(ld["gate"], 16)
            largest(GA, rawg[:, :, :], AX.XY).then_inc(s_mx, 1)
            dve.wait_ge(ld["bqk"], 32)
            dve.wait_ge(s_qkv, 1)
            for m in range(KC):
                last = nc.vector.tensor_scalar(qT[:, m], psU[0][:, m * P:(m + 1) * P], bqk[:, 0, m:m + 1], float(HD) ** -0.5,
                                               ALU.add, ALU.mult)
            last.then_inc(s_qk, 1)
            dve.wait_ge(s_qkv, 2)
            for m in range(KC):
                last = nc.vector.tensor_scalar(kT[:, m], psU[1][:, m * P:(m + 1) * P], bqk[:, 1, m:m + 1], None, ALU.add)
            last.then_inc(s_qk, 1)
            scales(WO, GA + 1, 1)
            dve.wait_ge(s_qkv, 3)
            dve.wait_ge(ld["bv"], 16)
            link(nc.vector.tensor_tensor(val[:, :], psT[:, :], bv_sb, ALU.add))
            link(largest(VL, val[:, :], AX.X))
            link(largest(TK, tok[:, :], AX.X))
            dve.wait_ge(s_tab, 1)
            for j in range(4):
                link(nc.vector.tensor_reduce(mxs[:, j:j + 1], bank[j][:, :], AX.X, ALU.max, apply_absolute_value=True))
            largest(SC, mxs[:, :], AX.X).then_inc(s_mx, 1)
            low(wo_hl[:, 1], raww, wo_hl[:, 0], WO)
            low(ex_hl[:, 1], rawe, ex_hl[:, 0], EX)
            low(gt_hl[:, 1], rawg[:, :, :], gt_hl[:, 0], GA)
            scales(SC, VL + 1, 2)
            nc.vector.tensor_scalar(val[:, :], val[:, :], scl[:, VL:VL + 1], None, ALU.mult).then_inc(s_val, 1)
            for j in range(4):
                low(sc_hl[:, 1].rearrange("p (c j) v -> p c j v", j=4)[:, :, j, :],
                    bank[j][:, :].rearrange("p (c v) -> p c v", v=P),
                    sc_hl[:, 0].rearrange("p (c j) v -> p c j v", j=4)[:, :, j, :], SC)
            low(tk_hl[:, 1], tok[:, :], tk_hl[:, 0], TK)
            link(nc.vector.tensor_scalar(kap[:, KO:KO + 1], inv[:, VL:VL + 1], inv[:, WO:WO + 1], None, ALU.mult))
            link(nc.vector.tensor_scalar(kap[:, KE:KE + 1], inv[:, GA:GA + 1], inv[:, EX:EX + 1], 2.0 ** (-2 * XSHIFT),
                                         ALU.mult, ALU.mult))

            def carry_wait():
                nc.vector.tensor_copy(carrier[:, :], half[:, 0:1])

            def bias_and_max(u, g):
                tile = g * TILES + u % TILES
                dve.wait_ge(s_scored, g * UNITS + u + 1)
                if u >= 2:
                    dve.wait_ge(s_exp, g * UNITS + u - 1)
                nc.vector.scalar_tensor_tensor(
                    tadd[:, u % 2], psS[:, :].rearrange("p (h v) -> p h v", h=4), inv[:, SC:SC + 1],
                    lnc[:, bass.ds(tile, 1), :].broadcast_to([P, 4, P]), ALU.mult, ALU.add).then_inc(s_added, 1)
                dve.wait_ge(s_added, g * UNITS + u + 1)
                nc.vector.tensor_reduce(nmax[:, u % 2], tadd[:, u % 2], AX.X, ALU.max, negate=True).then_inc(s_max, 1)

            def normalise(u, g):
                dve.wait_ge(s_exp, g * UNITS + u + 1)
                nc.vector.reciprocal(rinv[:, u % 2], rsum[:, u % 2]).then_inc(s_rec, 1)
                dve.wait_ge(s_rec, g * UNITS + u + 1)
                nc.vector.tensor_tensor(prob[:, u % 2], prob[:, u % 2],
                                        rinv[:, u % 2].unsqueeze(2).broadcast_to([P, 4, P]), ALU.mult).then_inc(s_norm, 1)

            def low_y(q, g):
                dve.wait_ge(s_yh, g * HQ + q + 1)
                nc.vector.tensor_tensor(yt_hl[:, 1, q], psT[:, :], yt_hl[:, 0, q], ALU.subtract).then_inc(s_yl, 1)

            def residual(j, g):
                dve.wait_ge(s_wo, g * TILES + j + 1)
                dve.wait_ge(s_tokr, g * TILES + j + 1)
                need(dve, s_h1b, g * TILES)
                nc.vector.scalar_tensor_tensor(h1[:, j], psT[:, :], kap[:, KO:KO + 1], tokr[:, j % 2], ALU.mult,
                                               ALU.add).then_inc(s_h1, 1)
                dve.wait_ge(s_h1, g * TILES + j + 1)
                nc.vector.bn_stats(bnx[:, j], h1[:, j]).then_inc(s_bn, 1)
                dve.wait_ge(s_bn, g * TILES + j + 1)
                carry_wait()
                nc.vector.bn_aggr(mvx[:, j], bnx[:, j]).then_inc(s_agg, 1)
                dve.wait_ge(s_agg, g * TILES + j + 1)
                nc.vector.tensor_scalar(vex[:, j:j + 1], mvx[:, j, 1:2], EPS_LN, 2.0 ** (-2 * XSHIFT), ALU.add,
                                        ALU.mult).then_inc(s_ve, 1)

            def layer_norm(j, g):
                dve.wait_ge(s_rs, g * TILES + j + 1)
                if j >= 2:
                    dve.wait_ge(s_xt, g * TILES + j - 1)
                nc.vector.tensor_scalar(xrow[:, j % 2], h1[:, j], mvx[:, j, 0:1], rsx[:, j:j + 1], ALU.subtract,
                                        ALU.mult).then_inc(s_x, 1)

            def low_x(j, g, b):
                dve.wait_ge(s_xh, g * TILES + j + 1)
                c = slice(j * P, (j + 1) * P)
                nc.vector.tensor_tensor(xt_hl[:, 1, :, c], psU[b][:, :].rearrange("p (k t) -> p k t", k=KC),
                                        xt_hl[:, 0, :, c], ALU.subtract).then_inc(s_xl, 1)

            def routing(g):
                dve.wait_ge(s_gate, g + 1)
                carry_wait()
                for j in range(TILES):
                    last = nc.vector.max(top8[:, j], psS[:, j * NEXP:(j + 1) * NEXP])
                last.then_inc(s_top, 1)
                dve.wait_ge(s_top, g + 1)
                for j in range(TILES):
                    last = nc.vector.tensor_scalar(rout[:, j:j + 1], top8[:, j, 0:1], top8[:, j, 1:2], kap[:, KE:KE + 1],
                                                   ALU.add, ALU.mult)
                last.then_inc(s_rout, 1)

            def low_square(i, g):
                dve.wait_ge(s_sh, g * IC + i + 1)
                nc.vector.tensor_tensor(sq_hl[:, i % RING, 1], sqr[:, i % 2], sq_hl[:, i % RING, 0],
                                        ALU.subtract).then_inc(s_sl, 1)

            def expert_rows(j, g):
                if j == 0:
                    dve.wait_ge(s_rout, g + 1)
                dve.wait_ge(s_ex, g * TILES + j + 1)
                nc.vector.tensor_scalar(y[:, j], psU[EXPERT_BANK[j]][:, :], rout[:, j:j + 1], None, ALU.mult).then_inc(s_moe, 1)

            def finish(g):
                dve.wait_ge(s_dn, (g + 1) * IC)
                for j in range(TILES):
                    dve.wait_ge(s_moe, g * TILES + j + 1)
                    nc.vector.scalar_tensor_tensor(y[:, j], psY[j][:, :], kap[:, KY:KY + 1], y[:, j], ALU.mult,
                                                   ALU.add).then_inc(s_yev, 1)
                for j in range(TILES):
                    dve.wait_ge(s_yev, g * TILES + j + 1)
                    nc.vector.bn_stats(bny[:, j], y[:, j]).then_inc(s_bny, 1)
                dve.wait_ge(s_bny, (g + 1) * TILES)
                carry_wait()
                for j in range(TILES):
                    last = nc.vector.bn_aggr(mvy[:, j], bny[:, j])
                last.then_inc(s_aggy, 1)
                dve.wait_ge(s_aggy, g + 1)
                nc.vector.tensor_scalar(vey[:, :], mvy[:, :, 1], EPS_LN, None, ALU.add).then_inc(s_vey, 1)
                for j in range(TILES):
                    nc.vector.scalar_tensor_tensor(y[:, j], y[:, j], mvy[:, j, 0:1], gam, ALU.subtract,
                                                   ALU.mult).then_inc(s_z, 1)
                dve.wait_ge(s_rsy, g + 1)
                for j in range(TILES):
                    dve.wait_ge(s_z, g * TILES + j + 1)
                    dve.wait_ge(s_h1b, g * TILES + j + 1)
                    need(dve, s_out[j % 2], g * (8 * TILES) + (j // 2 + 1) * 16)
                    nc.vector.scalar_tensor_tensor(fin[:, j % 2], y[:, j], rsy[:, j:j + 1], h1b[:, j], ALU.mult,
                                                   ALU.add).then_inc(s_fin, 1)

            bias_and_max(0, 0)
            for u in range(UNITS):
                if u < UNITS - 1:
                    bias_and_max(u + 1, 0)
                normalise(u, 0)
                if u % TILES == TILES - 1:
                    low_y(u // TILES, 0)
            dve.wait_ge(ld["up"], 16)
            largest(UP, rawu[:, :], AX.X).then_inc(s_mx, 1)
            dve.wait_ge(ld["dn"], 16)
            largest(DN, rawd[:, :], AX.X).then_inc(s_mx, 1)
            scales(UP, UP + 1, 3)
            scales(DN, DN + 1, 4)
            for k in range(KC):
                low(up_hl[:, 1, k], rawu[:, k * INTER:(k + 1) * INTER], up_hl[:, 0, k], UP)
            for k in range(4):
                low(dn_hl[:, 1, 4 * k:4 * k + 4], rawd[:, k * 2048:(k + 1) * 2048].rearrange("p (k n) -> p k n", k=4),
                    dn_hl[:, 0, 4 * k:4 * k + 4], DN)
            link(nc.vector.tensor_scalar(kap[:, KY:KY + 1], inv[:, UP:UP + 1], 2.0 ** RSHIFT, None, ALU.mult))
            link(nc.vector.tensor_scalar(kap[:, KY:KY + 1], kap[:, KY:KY + 1], kap[:, KY:KY + 1], inv[:, DN:DN + 1],
                                         ALU.mult, ALU.mult))
            residual(0, 0)
            layer_norm(0, 0)
            residual(1, 0)
            low_x(0, 0, 1)
            layer_norm(1, 0)
            residual(2, 0)
            layer_norm(2, 0)
            low_x(1, 0, 1)
            residual(3, 0)
            layer_norm(3, 0)
            low_x(2, 0, 0)
            low_x(3, 0, 1)
            dve.wait_ge(ld["gam"], 32)
            with dve.Fori(0, GROUPS - 1) as g:
                routing(g)
                for i in range(IC):
                    if i > 0:
                        normalise(i - 1, g + 1)
                    bias_and_max(i, g + 1)
                    low_square(i, g)
                    if i > 0 and (i - 1) % TILES == TILES - 1:
                        low_y((i - 1) // TILES, g + 1)
                normalise(UNITS - 1, g + 1)
                expert_rows(0, g)
                low_y(HQ - 1, g + 1)
                expert_rows(1, g)
                residual(0, g + 1)
                expert_rows(2, g)
                layer_norm(0, g + 1)
                residual(1, g + 1)
                low_x(0, g + 1, 1)
                layer_norm(1, g + 1)
                expert_rows(3, g)
                residual(2, g + 1)
                layer_norm(2, g + 1)
                low_x(1, g + 1, 1)
                residual(3, g + 1)
                layer_norm(3, g + 1)
                low_x(2, g + 1, 0)
                low_x(3, g + 1, 1)
                finish(g)
            routing(GROUPS - 1)
            for i in range(IC):
                low_square(i, GROUPS - 1)
            for j in range(TILES):
                expert_rows(j, GROUPS - 1)
            finish(GROUPS - 1)

        @block.tensor
        def _(pe):
            mm = nc.tensor.matmul

            def split_product(dst, stat_hl, mov_hl, n, steps, start=True, stop=True):
                for k in range(steps):
                    for a, b in ((0, 0), (0, 1), (1, 0)):
                        last = mm(dst, stat_hl(a, k), mov_hl(b, k), start=start and k == 0 and a == b,
                                  stop=stop and k == steps - 1 and a == 1)
                return last

            pe.wait_ge(s_pool0, 5)
            pe.wait_ge(s_ohr, 1)
            for j in range(SEQ // P):
                dst = bank[j // 4][:, (j % 4) * P:(j % 4 + 1) * P]
                for i in range(j):
                    mm(dst, ones[:, :], ohr[:, i, :], start=i == 0, stop=False)
                last = mm(dst, tri[:, :], ohr[:, j, :], start=j == 0, stop=True)
                if j % 4 == 3:
                    last.then_inc(s_cnt, 1)
            for n in range(2):
                pe.wait_ge(s_row, n + 1)
                for k in range(KC):
                    last = nc.tensor.transpose(psS[:, k * P:(k + 1) * P], row[:, k * P:(k + 1) * P], ident[:, :])
                last.then_inc(s_rowT, 1)
                pe.wait_ge(s_colT, n + 1)
                if n == 0:
                    pe.wait_ge(ld["proj"], 16)
                    for k in range(KC):
                        last = mm(psT[:, :], colT[:, k], pj_sb[:, k], start=k == 0, stop=k == KC - 1)
                    last.then_inc(s_proj, 1)
            for i, w in enumerate((wq_sb, wk_sb)):
                pe.wait_ge(ld["wq" if i == 0 else "wk"], 16)
                for m in range(KC):
                    for k in range(KC):
                        last = mm(psU[i][:, m * P:(m + 1) * P], w[:, k, m * P:(m + 1) * P], colT[:, k],
                                  start=k == 0, stop=k == KC - 1)
                last.then_inc(s_qkv, 1)
            pe.wait_ge(ld["wv"], 16)
            for k in range(KC):
                last = mm(psT[:, :], colT[:, k], wv_sb[:, k], start=k == 0, stop=k == KC - 1)
            last.then_inc(s_qkv, 1)
            pe.wait_ge(s_qk, 2)
            pe.wait_ge(s_lnc, 4)
            for c in range(KC):
                for j in range(4):
                    r = slice(HD * j, HD * (j + 1))
                    last = mm(bank[j][:, c * P:(c + 1) * P], qT[r, c, :], kT[r, c, :], start=True, stop=True)
            last.then_inc(s_tab, 1)

            def score(u, g):
                q, j = u // TILES, u % TILES
                need(pe, s_added, g * UNITS + u)
                if u == 0:
                    need(pe, s_tokr, g * TILES)
                t = bass.ds(g * GT + j * P, P)
                for a in range(2):
                    last = mm(psS[:, :], oht[:, t], sc_hl[:, a, 4 * q:4 * q + 4, :].rearrange("p h v -> p (h v)"),
                              start=a == 0, stop=a == 1)
                last.then_inc(s_scored, 1)

            def transpose_probs(u, g):
                pe.wait_ge(s_norm, g * UNITS + u + 1)
                need(pe, s_pt, g * UNITS + u)
                if u % TILES == 0 and u > 0:
                    pe.wait_ge(s_yl, g * HQ + u // TILES)
                if u == 0:
                    need(pe, s_h1, g * TILES)
                for h in range(4):
                    last = nc.tensor.transpose(psT[:, h * P:(h + 1) * P], prob[:, u % 2, h, :], ident[:, :])
                last.then_inc(s_trn, 1)

            def attend(q, g):
                pe.wait_ge(s_pt, g * UNITS + (q + 1) * TILES)
                for h in range(4):
                    c = (4 * q + h) * HD
                    last = mm(psT[HD * h:HD * (h + 1), :], val[:, c:c + HD], probT[:, q % 2, h, :],
                              start=True, stop=True)
                last.then_inc(s_pv, 1)

            def attention_out(j, g):
                if j == 0:
                    pe.wait_ge(s_yl, (g + 1) * HQ)
                    pe.wait_ge(s_added, (g + 1) * UNITS)
                else:
                    pe.wait_ge(s_tokr, g * TILES + j)
                    pe.wait_ge(s_h1, g * TILES + j)
                t = bass.ds(g * GT + j * P, P)
                for a in range(2):
                    last = mm(psS[:, :], oht[:, t], tk_hl[:, a], start=a == 0, stop=a == 1)
                last.then_inc(s_tg, 1)
                c = slice(j * P, (j + 1) * P)
                split_product(psT[:, :], lambda a, k: yt_hl[:, a, k, c], lambda b, k: wo_hl[:, b, k], DM,
                              KC).then_inc(s_wo, 1)

            def transpose_rows(j, g, b, bank_free):
                pe.wait_ge(s_x, g * TILES + j + 1)
                if bank_free is not None:
                    need(pe, *bank_free)
                for k in range(KC):
                    last = nc.tensor.transpose(psU[b][:, k * P:(k + 1) * P], xrow[:, j % 2, k * P:(k + 1) * P],
                                               ident[:, :])
                last.then_inc(s_xt, 1)

            def gate_logits(g):
                pe.wait_ge(s_xl, (g + 1) * TILES)
                pe.wait_ge(s_tokr, (g + 1) * TILES)
                for j in range(TILES):
                    c = slice(j * P, (j + 1) * P)
                    last = split_product(psS[:, j * NEXP:(j + 1) * NEXP], lambda a, k: xt_hl[:, a, k, c],
                                         lambda b, k: gt_hl[:, b, k, :], NEXP, KC)
                last.then_inc(s_gate, 1)

            def up_chunk(i, g):
                if i >= 2:
                    pe.wait_ge(s_relu, g * IC + i - 1)
                c = slice(i * P, (i + 1) * P)
                split_product(psU[i % 2][:, :], lambda a, k: up_hl[:, a, k, c], lambda b, k: xt_hl[:, b, k, :], GT,
                              KC).then_inc(s_up, 1)

            def down_chunk(i, g):
                pe.wait_ge(s_sl, g * IC + i + 1)
                for j in range(TILES):
                    c = slice(j * P, (j + 1) * P)
                    last = split_product(psY[j][:, :], lambda a, k: sq_hl[:, i % RING, a, c],
                                         lambda b, k: dn_hl[:, b, i], DM, 1, start=i == 0, stop=i == IC - 1)
                last.then_inc(s_dn, 1)

            def expert_product(j, g):
                if j < 2:
                    pe.wait_ge(s_relu, g * IC + IC - 1 + j)
                else:
                    pe.wait_ge(s_moe, g * TILES + 2 * j - 3)
                c = slice(j * P, (j + 1) * P)
                split_product(psU[EXPERT_BANK[j]][:, :], lambda a, k: xt_hl[:, a, k, c], lambda b, k: ex_hl[:, b, k], DM,
                              KC).then_inc(s_ex, 1)

            pe.wait_ge(s_oht, 4)
            pe.wait_ge(s_lo, 8)
            pe.wait_ge(s_val, 1)
            score(0, 0)
            for u in range(UNITS):
                if u < UNITS - 1:
                    score(u + 1, 0)
                transpose_probs(u, 0)
                if u % TILES == TILES - 1:
                    attend(u // TILES, 0)
            attention_out(0, 0)
            attention_out(1, 0)
            transpose_rows(0, 0, 1, None)
            attention_out(2, 0)
            transpose_rows(1, 0, 1, (s_xl, 1))
            attention_out(3, 0)
            transpose_rows(2, 0, 0, None)
            transpose_rows(3, 0, 1, (s_xl, 2))
            pe.wait_ge(s_lo, 16)
            with pe.Fori(0, GROUPS - 1) as g:
                gate_logits(g)
                for i in range(IC):
                    up_chunk(i, g)
                    if i == 0:
                        pe.wait_ge(s_rout, g + 1)
                    score(i, g + 1)
                    if i > 0:
                        transpose_probs(i - 1, g + 1)
                        down_chunk(i - 1, g)
                        if (i - 1) % TILES == TILES - 1:
                            attend((i - 1) // TILES, g + 1)
                transpose_probs(UNITS - 1, g + 1)
                expert_product(0, g)
                attend(HQ - 1, g + 1)
                expert_product(1, g)
                attention_out(0, g + 1)
                expert_product(2, g)
                attention_out(1, g + 1)
                transpose_rows(0, g + 1, 1, (s_moe, g * TILES + 2))
                expert_product(3, g)
                attention_out(2, g + 1)
                transpose_rows(1, g + 1, 1, (s_xl, g * TILES + TILES + 1))
                attention_out(3, g + 1)
                transpose_rows(2, g + 1, 0, (s_moe, g * TILES + 4))
                down_chunk(IC - 1, g)
                transpose_rows(3, g + 1, 1, (s_xl, g * TILES + TILES + 2))
            gate_logits(GROUPS - 1)
            for i in range(IC):
                up_chunk(i, GROUPS - 1)
                if i == 0:
                    pe.wait_ge(s_rout, GROUPS)
                if i > 0:
                    down_chunk(i - 1, GROUPS - 1)
            for j in range(TILES):
                expert_product(j, GROUPS - 1)
            down_chunk(IC - 1, GROUPS - 1)


def kernel(x, L0_tok_emb_table, L0_tok_norm_weight, L0_tok_proj_weight, L0_attn_Wq, L0_attn_bq, L0_attn_Wk,
           L0_attn_bk, L0_attn_Wv, L0_attn_bv, L0_attn_Wo, L0_attn_bo, L0_ffn_gate_w, L0_ffn_up_w, L0_ffn_down_w,
           L0_ffn_expert_weight, L0_ffn_ln_gamma, L0_ffn_ln_beta):
    import numpy as np
    import concourse.bacc as bacc
    from concourse.bass_utils import run_bass_kernel_spmd

    def heads_last(w):
        return np.asarray(w).transpose(1, 0, 2).reshape(DM, DM)

    def column(b):
        return np.asarray(b).reshape(KC, P).T

    given = {
        "ids": np.asarray(x).reshape(SEQ), "ids_col": np.asarray(x).reshape(SEQ // P, P).T, "emb": L0_tok_emb_table, "norm_w": L0_tok_norm_weight,
        "proj_t": np.asarray(L0_tok_proj_weight).T, "wq": heads_last(L0_attn_Wq), "wk": heads_last(L0_attn_Wk),
        "wv": heads_last(L0_attn_Wv), "bq": column(L0_attn_bq), "bk": column(L0_attn_bk),
        "bv": np.asarray(L0_attn_bv).reshape(DM), "wo": L0_attn_Wo, "bo": L0_attn_bo, "up": L0_ffn_up_w,
        "down": L0_ffn_down_w, "expert": L0_ffn_expert_weight, "gate": L0_ffn_gate_w, "gamma": L0_ffn_ln_gamma,
        "beta": L0_ffn_ln_beta,
    }
    nc = bacc.Bacc("TRN2", target_bir_lowering=False, num_devices=1)
    arrays, aps = {}, {}
    for name, a in given.items():
        a = np.ascontiguousarray(a)
        arrays[f"in_{name}"] = a
        aps[name] = nc.dram_tensor(f"in_{name}", a.shape, mybir.dt.from_np(a.dtype), kind="ExternalInput").ap()
    out = nc.dram_tensor("out_rows", (SEQ, DM), F32, kind="ExternalOutput").ap()
    tower(nc, out=out, **aps)
    got = run_bass_kernel_spmd(nc, [arrays], core_ids=[0]).results[0]["out_rows"]
    return got.reshape(1, SEQ, DM)
```

```python
import concourse.bass as bass
from concourse import mybir
from contextlib import ExitStack

F32 = mybir.dt.float32
F16 = mybir.dt.float16
I32 = mybir.dt.int32
ALU = mybir.AluOpType
ACT = mybir.ActivationFunctionType
AX = mybir.AxisListType
ABSMAX = bass.bass_isa.ReduceOp.absmax

P = 128
SEQ = 2048
DM = 512
KC = DM // P
HEADS = 16
HD = DM // HEADS
INTER = 2048
IC = INTER // P
NEXP = 8
GT = 512
GROUPS = SEQ // GT
TILES = GT // P
HQ = HEADS // 4
UNITS = HQ * TILES
UBUF = 4
RING = 3

EXPERT_BANK = (0, 1, 0, 0)
TOP = 14
XSHIFT = 11
RSHIFT = 17
TINY = 1e-18
UNSEEN = 1e28
EPS_RMS = 1e-6
EPS_LN = 1e-5


def tower(nc, ids_col, emb, norm_w, proj_t, wq, wk, wv, bq, bk, bv, wo, bo, up, down, expert, gate, gamma, beta, out):
    ctx = ExitStack()
    with ctx:
        def sb(name, shape, dt):
            return ctx.enter_context(nc.sbuf_tensor(name, shape, dt))

        def sem(name):
            return ctx.enter_context(nc.semaphore(name))

        wo_hl = sb("wo_hl", [P, 2, KC, DM], F16)
        up_hl = sb("up_hl", [P, 2, KC, INTER], F16)
        ex_hl = sb("ex_hl", [P, 2, KC, DM], F16)
        dn_hl = sb("dn_hl", [P, 2, IC, DM], F16)
        gt_hl = sb("gt_hl", [P, 2, KC, NEXP], F16)
        sc_hl = sb("sc_hl", [P, 2, HEADS, P], F16)
        tk_hl = sb("tk_hl", [P, 2, DM], F16)
        oht = sb("oht", [P, SEQ], F16)
        lnc = sb("lnc", [P, SEQ // P, P], F32)
        val = sb("val", [P, DM], F32)
        prob = sb("prob", [P, UBUF, 4, P], F32)
        probT = sb("probT", [P, 2, 4, GT], F32)
        yt_hl = sb("yt_hl", [P, 2, HQ, GT], F16)
        rawu = sb("rawu", [P, KC * INTER], F32)
        tokr = rawu[:, 0:1024].rearrange("p (b n) -> p b n", b=2)
        xrow = rawu[:, 1024:2048].rearrange("p (b n) -> p b n", b=2)
        h1 = rawu[:, 2048:4096].rearrange("p (j n) -> p j n", j=TILES)
        h1b = rawu[:, 4096:6144].rearrange("p (j n) -> p j n", j=TILES)
        xt_hl = rawu[:, 6144:8192].bitcast(F16).rearrange("p (a k t) -> p a k t", a=2, k=KC)
        rawd = sb("rawd", [P, IC * DM], F32)
        relu = rawd[:, 0:1024].rearrange("p (b n) -> p b n", b=2)
        sqr = rawd[:, 1024:2048].rearrange("p (b n) -> p b n", b=2)
        y = rawd[:, 2048:4096].rearrange("p (j n) -> p j n", j=TILES)
        fin = rawd[:, 4096:5120].rearrange("p (b n) -> p b n", b=2)
        sq_hl = rawd[:, 5120:5120 + RING * DM].bitcast(F16).rearrange("p (b a n) -> p b a n", b=RING, a=2)
        gam = rawd[:, 5120 + RING * DM:5120 + RING * DM + DM]
        bet = rawd[:, 5120 + RING * DM + DM:5120 + RING * DM + 2 * DM]
        raww = yt_hl[:, :, :, :].rearrange("p a k n -> p (a k n)").bitcast(F32).rearrange("p (k n) -> p k n", k=KC)
        rawe = probT[:, 1]
        wflat = dn_hl[:, :, :, :].rearrange("p a k n -> p (a k n)").bitcast(F32).rearrange("p (w k n) -> p w k n", w=4, k=KC)
        pj_sb, wq_sb, wk_sb, wv_sb = (wflat[:, i] for i in range(4))
        exf = ex_hl[:, :, :, :].rearrange("p a k n -> p (a k n)")
        ohr = exf[:, 0:2048].rearrange("p (j v) -> p j v", v=P)
        unseen = exf[:, 2048:3072].bitcast(F32)
        pflat = prob[:, :, :, :].rearrange("p b j v -> p (b j v)")
        row = pflat[:, 0:DM]
        nrm = pflat[:, DM:2 * DM]
        colT = pflat[:, 2 * DM:3 * DM].rearrange("p (k v) -> p k v", k=KC)
        kT = pflat[:, 3 * DM:4 * DM].rearrange("p (k v) -> p k v", k=KC)
        tok = sb("tok", [P, DM], F32)
        sflat = sc_hl[:, :, :, :].rearrange("p a h v -> p (a h v)").bitcast(F32)
        bo_sb = sflat[:, 0:DM]
        bv_sb = sflat[:, DM:2 * DM]
        qT = sflat[:, 2 * DM:3 * DM].rearrange("p (k v) -> p k v", k=KC)
        iota_v = sflat[:, 3 * DM:3 * DM + P]
        iota_vi = sflat[:, 3 * DM + P:3 * DM + 2 * P].bitcast(I32)
        identh = sflat[:, 3 * DM + 2 * P:3 * DM + 2 * P + P // 2].bitcast(F16)
        ident = sb("ident", [P, P], F32)
        tri = sb("tri", [P, P], F16)
        ones = sb("ones", [P, P], F16)
        lnb = sb("lnb", [P, 2], F32)
        idc = sb("idc", [P, SEQ // P], F32)
        tmpc2 = sb("tmpc2", [P, SEQ // P], F32)
        tmpc = sb("tmpc", [P, SEQ // P], F32)
        bqk = sb("bqk", [P, 2, KC], F32)
        rawg = sb("rawg", [P, KC, NEXP], F32)
        mxs = sb("mxs", [P, 4], F32)
        ssq = sb("ssq", [P, 4], F32)
        ams = sb("ams", [P, 4], F32)
        mx = sb("mx", [P, 8], F32)
        am = sb("am", [P, 8], F32)
        p2 = sb("p2", [P, 8], F32)
        inv = sb("inv", [P, 8], F32)
        scl = sb("scl", [P, 8], F32)
        kap = sb("kap", [P, 4], F32)
        stat = sb("stat", [P, 2, 8], F32)
        bn0 = sb("bn0", [P, 6], F32)
        carrier = sb("carrier", [P, 1], F32)
        root = sb("root", [P, 4], F32)
        ssw = sb("ssw", [P, 2], F32)
        amw = sb("amw", [P, 2], F32)
        nmean = sb("nmean", [P, TILES], F32)
        half = sb("half", [P, TILES], F32)
        nmax = sb("nmax", [P, UBUF, 4], F32)
        rsum = sb("rsum", [P, UBUF, 4], F32)
        rinv = sb("rinv", [P, UBUF, 4], F32)
        bnx = sb("bnx", [P, TILES, 6], F32)
        mvx = sb("mvx", [P, TILES, 2], F32)
        vex = sb("vex", [P, TILES], F32)
        rsx = sb("rsx", [P, TILES], F32)
        bny = sb("bny", [P, TILES, 6], F32)
        mvy = sb("mvy", [P, TILES, 2], F32)
        vey = sb("vey", [P, TILES], F32)
        rsy = sb("rsy", [P, TILES], F32)
        top8 = sb("top8", [P, TILES, 8], F32)
        rout = sb("rout", [P, TILES], F32)
        nbias = sb("nbias", [P, TILES], F32)
        SC, TK, VL, WO, EX, GA, UP, DN = range(8)
        KO, KE, KY = range(3)

        bank = [ctx.enter_context(nc.psum_tensor(f"bank{i}", [P, 512], F32)) for i in range(8)]
        psY, psU, psS, psT = bank[0:4], bank[4:6], bank[6], bank[7]

        ld = {n: sem("ld_" + n) for n in ("idc", "emb", "nw", "proj", "wq", "wk", "wv", "bqk", "bv", "bo",
                                          "wo", "up0", "up1", "up2", "up3", "gate", "ex", "dn", "gam")}
        s_iota, s_pool0, s_dve, s_act = sem("s_iota"), sem("s_pool0"), sem("s_dve"), sem("s_act")
        s_ohr, s_cnt, s_lnraw, s_unseen, s_lnc = (sem(n) for n in ("s_ohr", "s_cnt", "s_lnraw", "s_unseen", "s_lnc"))
        s_var0, s_rs0, s_row, s_rowT, s_colT, s_proj, s_psb = (sem(n) for n in (
            "s_var0", "s_rs0", "s_row", "s_rowT", "s_colT", "s_proj", "s_psb"))
        s_qkv, s_qk, s_tab, s_ohT, s_oht = sem("s_qkv"), sem("s_qk"), sem("s_tab"), sem("s_ohT"), sem("s_oht")
        s_vsum, s_ssq, s_ams, s_ssw, s_amw = (sem(n) for n in ("s_vsum", "s_ssq", "s_ams", "s_ssw", "s_amw"))
        s_mx, s_am, s_scl = sem("s_mx"), sem("s_am"), sem("s_scl")
        s_hi, s_lo, s_val = sem("s_hi"), sem("s_lo"), sem("s_val")
        s_whi, s_wlo, s_uphi, s_uplo, s_dnhi, s_dnlo = (sem(n) for n in (
            "s_whi", "s_wlo", "s_uphi", "s_uplo", "s_dnhi", "s_dnlo"))
        s_scored, s_added, s_max, s_exp, s_rec, s_norm, s_trn, s_pt = (sem(n) for n in (
            "s_scored", "s_added", "s_max", "s_exp", "s_rec", "s_norm", "s_trn", "s_pt"))
        s_pv, s_yh, s_yl = sem("s_pv"), sem("s_yh"), sem("s_yl")
        s_tg, s_wo, s_tokr, s_h1, s_bn, s_agg, s_ve, s_rs, s_x, s_xt, s_xh, s_xl, s_h1b = (sem(n) for n in (
            "s_tg", "s_wo", "s_tokr", "s_h1", "s_bn", "s_agg", "s_ve", "s_rs", "s_x", "s_xt", "s_xh", "s_xl", "s_h1b"))
        s_gate, s_top, s_rout, s_up, s_relu, s_sq, s_sh, s_sl, s_dn, s_ex, s_moe = (sem(n) for n in (
            "s_gate", "s_top", "s_rout", "s_up", "s_relu", "s_sq", "s_sh", "s_sl", "s_dn", "s_ex", "s_moe"))
        s_dt, s_yev, s_bny, s_aggy, s_vey, s_rsy, s_nb, s_zn, s_zg, s_fin = (sem(n) for n in (
            "s_dt", "s_yev", "s_bny", "s_aggy", "s_vey", "s_rsy", "s_nb", "s_zn", "s_zg", "s_fin"))
        s_out = [sem("s_out0"), sem("s_out1")]

        def need(eng, s, value):
            if isinstance(value, int) and value <= 0:
                return
            eng.wait_ge(s, value)

        def bc(ap, n, dt_shape):
            return ap.unsqueeze(1).broadcast_to(dt_shape)

        block = ctx.enter_context(nc.Block())

        @block.sync
        def _(sp):
            for b in range(2):
                sp.sem_inc(s_out[b], 16)

            def load(dst, src, name):
                sp.dma_start(dst, src).then_inc(ld[name], 16)

            load(row, emb, "emb")
            load(idc[:, :].bitcast(I32), ids_col, "idc")
            load(nrm, norm_w.partition_broadcast(P), "nw")
            load(pj_sb, proj_t.rearrange("(k p) n -> p k n", p=P), "proj")
            load(wq_sb, wq.rearrange("(k p) n -> p k n", p=P), "wq")
            load(bqk[:, 0], bq, "bqk")
            load(bqk[:, 1], bk, "bqk")
            load(wk_sb, wk.rearrange("(k p) n -> p k n", p=P), "wk")
            load(wv_sb, wv.rearrange("(k p) n -> p k n", p=P), "wv")
            load(bv_sb, bv.partition_broadcast(P), "bv")
            load(bo_sb, bo.partition_broadcast(P), "bo")
            for k in range(KC):
                load(rawu[:, k * INTER:(k + 1) * INTER], up[k * P:(k + 1) * P, :], f"up{k}")
            load(raww, wo.rearrange("(k p) n -> p k n", p=P), "wo")
            load(rawe, expert.rearrange("(k p) n -> p k n", p=P), "ex")
            load(rawg[:, :, :], gate.rearrange("(k p) n -> p k n", p=P), "gate")
            load(rawd[:, :].rearrange("p (k n) -> p k n", k=IC), down.rearrange("(k p) n -> p k n", p=P), "dn")
            sp.wait_ge(s_dnlo, 4)
            load(gam, gamma.partition_broadcast(P), "gam")
            load(bet, beta.partition_broadcast(P), "gam")

            def store(g):
                for j in range(TILES):
                    sp.wait_ge(s_fin, g * TILES + j + 1)
                    sp.dma_start(out[bass.ds(g * GT + j * P, P), :], fin[:, j % 2]).then_inc(s_out[j % 2], 16)

            with sp.Fori(0, GROUPS) as g:
                store(g)
            for b in range(2):
                sp.wait_ge(s_out[b], 16 * (GROUPS * TILES // 2 + 1))

        @block.gpsimd
        def _(pool):
            nc.gpsimd.iota(iota_vi, [[1, P]], base=0, channel_multiplier=0).then_inc(s_iota, 1)
            nc.gpsimd.memset(half[:, :], -0.5).then_inc(s_pool0, 1)
            nc.gpsimd.memset(root[:, :], 0.5).then_inc(s_pool0, 1)
            nc.gpsimd.memset(ident[:, :], 0.0).then_inc(s_pool0, 1)
            nc.gpsimd.memset(identh, 0.0).then_inc(s_pool0, 1)
            nc.gpsimd.memset(ones[:, :], 1.0).then_inc(s_pool0, 1)
            nc.gpsimd.memset(lnb[:, 0:1], TINY).then_inc(s_pool0, 1)
            nc.gpsimd.memset(lnb[:, 1:2], -10 * UNSEEN).then_inc(s_pool0, 1)
            pool.wait_ge(s_pool0, 7)
            for m in (ident[:, :], identh):
                nc.gpsimd.affine_select(out=m, in_=m, compare_op=ALU.not_equal, fill=1.0, base=0,
                                        pattern=[[-1, P]], channel_multiplier=1).then_inc(s_pool0, 1)
            nc.gpsimd.affine_select(out=tri[:, :], in_=ones[:, :], compare_op=ALU.is_ge, fill=0.0, base=0,
                                    pattern=[[1, P]], channel_multiplier=-1).then_inc(s_pool0, 1)

            def rsqrt(dst, src, n):
                return nc.gpsimd.tensor_tensor(dst, src, half[:, 0:n], ALU.pow)

            def all_largest(dst, src, n):
                pool.wait_ge(s_mx, n)
                nc.gpsimd.partition_all_reduce(dst, src, P, ABSMAX).then_inc(s_am, 1)

            for i in range(3):
                pool.wait_ge(s_var0, i + 1)
                rsqrt(stat[:, 1, i:i + 1], stat[:, 0, i:i + 1], 1).then_inc(s_rs0, 1)
            all_largest(am[:, UP:UP + 1], mx[:, UP:UP + 1], 1)
            all_largest(am[:, SC:VL + 1], mx[:, SC:VL + 1], 2)

            def up_low(k):
                pool.wait_ge(s_uphi, k + 1)
                nc.gpsimd.tensor_tensor(up_hl[:, 1, k], rawu[:, k * INTER:(k + 1) * INTER], up_hl[:, 0, k],
                                        ALU.subtract).then_inc(s_uplo, 1)

            up_low(0)
            pool.wait_ge(s_mx, 3)
            nc.gpsimd.partition_all_reduce(am[:, GA:GA + 1], mx[:, GA:GA + 1], P, ABSMAX).then_inc(s_amw, 1)
            pool.wait_ge(s_ssw, 2)
            nc.gpsimd.partition_all_reduce(amw[:, :], ssw[:, :], P, ABSMAX).then_inc(s_amw, 1)
            pool.wait_ge(s_amw, 2)
            nc.gpsimd.tensor_tensor(am[:, WO:EX + 1], amw[:, :], root[:, 0:2], ALU.pow).then_inc(s_am, 1)
            for k in range(1, KC):
                up_low(k)
            pool.wait_ge(s_ssq, 4)
            nc.gpsimd.partition_all_reduce(ams[:, :], ssq[:, :], P, ABSMAX).then_inc(s_ams, 1)
            pool.wait_ge(s_ams, 1)
            nc.gpsimd.tensor_tensor(ams[:, 0:2], ams[:, 0:2], ams[:, 2:4], ALU.add).then_inc(s_ams, 1)
            pool.wait_ge(s_ams, 2)
            nc.gpsimd.tensor_tensor(ams[:, 0:1], ams[:, 0:1], ams[:, 1:2], ALU.add).then_inc(s_ams, 1)
            pool.wait_ge(s_ams, 3)
            nc.gpsimd.tensor_tensor(am[:, DN:DN + 1], ams[:, 0:1], root[:, 0:1], ALU.pow).then_inc(s_am, 1)
            for k in range(4):
                pool.wait_ge(s_dnhi, k + 1)
                nc.gpsimd.tensor_tensor(dn_hl[:, 1, 4 * k:4 * k + 4],
                                        rawd[:, k * 2048:(k + 1) * 2048].rearrange("p (k n) -> p k n", k=4),
                                        dn_hl[:, 0, 4 * k:4 * k + 4], ALU.subtract).then_inc(s_dnlo, 1)

            def row_norms(g):
                for j in range(TILES):
                    pool.wait_ge(s_ve, g * TILES + j + 1)
                    rsqrt(rsx[:, j:j + 1], vex[:, j:j + 1], 1).then_inc(s_rs, 1)

            def row_plus_beta(j, g):
                nc.gpsimd.tensor_tensor(h1b[:, j], h1[:, j], bet, ALU.add).then_inc(s_h1b, 1)

            def finish(j, g):
                pool.wait_ge(s_zn, g * TILES + j + 1)
                nc.gpsimd.tensor_tensor(y[:, j], y[:, j], gam, ALU.mult).then_inc(s_zg, 1)
                pool.wait_ge(s_zg, g * TILES + j + 1)
                pool.wait_ge(s_out[j % 2], g * (8 * TILES) + (j // 2 + 1) * 16)
                nc.gpsimd.tensor_tensor(fin[:, j % 2], y[:, j], h1b[:, j], ALU.add).then_inc(s_fin, 1)

            row_norms(0)
            pool.wait_ge(ld["gam"], 32)
            pool.wait_ge(s_h1, TILES)
            for j in range(TILES):
                row_plus_beta(j, 0)
            with pool.Fori(0, GROUPS - 1) as g:
                row_norms(g + 1)
                pool.wait_ge(s_vey, g + 1)
                rsqrt(rsy[:, :], vey[:, :], TILES).then_inc(s_rsy, 1)
                pool.wait_ge(s_rsy, g + 1)
                nc.gpsimd.tensor_tensor(nbias[:, :], nmean[:, :], rsy[:, :], ALU.mult).then_inc(s_nb, 1)
                for j in range(TILES):
                    finish(j, g)
                    pool.wait_ge(s_fin, g * TILES + j + 1)
                    row_plus_beta(j, g + 1)
            for j in range(TILES):
                pool.wait_ge(s_vey, GROUPS + j)
                rsqrt(rsy[:, j:j + 1], vey[:, j:j + 1], 1).then_inc(s_rsy, 1)

        @block.scalar
        def _(act):
            def copy(dst, src, scale=None):
                if scale is None:
                    return nc.scalar.copy(dst, src)
                return nc.scalar.activation(dst, src, ACT.Copy, scale=scale)

            act.wait_ge(s_rowT, 1)
            copy(colT, psS[:, :]).then_inc(s_colT, 1)
            act.wait_ge(s_proj, 1)
            copy(tok[:, :], psT[:, :]).then_inc(s_psb, 1)

            def ln_counts(b, src):
                dst = lnc[:, 4 * b:4 * b + 4, :].rearrange("p j v -> p (j v)")
                act.wait_ge(s_cnt, b + 1)
                nc.scalar.activation(dst, src[:, :], ACT.Ln, bias=lnb[:, 0:1]).then_inc(s_lnraw, 1)
                act.wait_ge(s_lnraw, b + 1)
                need(act, s_lnc, b)
                nc.scalar.activation(unseen, dst, ACT.Relu, bias=lnb[:, 1:2], scale=-UNSEEN).then_inc(s_unseen, 1)

            ln_counts(0, bank[0])
            ln_counts(1, bank[1])
            for b in range(2):
                act.wait_ge(s_ohT, b + 1)
                copy(oht[:, b * 1024:(b + 1) * 1024], psU[b][:, :].bitcast(F16)).then_inc(s_oht, 1)
            act.wait_ge(s_rowT, 2)
            copy(colT, psS[:, :]).then_inc(s_colT, 1)

            for n, (w, l) in enumerate(((raww, "wo"), (rawe, "ex"))):
                act.wait_ge(ld[l], 16)
                nc.scalar.activation(up_hl[:, 1, n], w.rearrange("p k n -> p (k n)"), ACT.Square,
                                     accum_out=ssw[:, n:n + 1]).then_inc(s_ssw, 1)

            def up_high(k):
                act.wait_ge(s_scl, 1)
                raw = rawu[:, k * INTER:(k + 1) * INTER]
                copy(up_hl[:, 0, k], raw, scl[:, UP:UP + 1])
                copy(raw, raw, scl[:, UP:UP + 1]).then_inc(s_uphi, 1)

            for k in range(3):
                up_high(k)
            act.wait_ge(s_scl, 2)
            for j in range(4):
                copy(sc_hl[:, 0].rearrange("p (c j) v -> p c j v", j=4)[:, :, j, :],
                     bank[j][:, :].rearrange("p (c v) -> p c v", v=P), scl[:, SC:SC + 1]).then_inc(s_hi, 1)
            copy(tk_hl[:, 0], tok[:, :], scl[:, TK:TK + 1]).then_inc(s_hi, 1)
            ln_counts(2, psS)
            ln_counts(3, psT)

            def output_high():
                act.wait_ge(s_scl, 3)
                copy(wo_hl[:, 0], raww, scl[:, WO:WO + 1]).then_inc(s_whi, 1)

            def expert_high():
                act.wait_ge(s_lnc, 4)
                copy(ex_hl[:, 0], rawe, scl[:, EX:EX + 1]).then_inc(s_whi, 1)
                copy(gt_hl[:, 0], rawg[:, :, :], scl[:, GA:GA + 1]).then_inc(s_whi, 1)

            def down_squares(k):
                act.wait_ge(ld["dn"], 16)
                nc.scalar.activation(dn_hl[:, 1, 4 * k:4 * k + 4].rearrange("p k n -> p (k n)"),
                                     rawd[:, k * 2048:(k + 1) * 2048], ACT.Square,
                                     accum_out=ssq[:, k:k + 1]).then_inc(s_ssq, 1)

            def exps(u, g):
                act.wait_ge(s_max, g * UNITS + u + 1)
                for h in range(4):
                    last = nc.scalar.activation(prob[:, u % UBUF, h, :], prob[:, u % UBUF, h, :], ACT.Exp,
                                                bias=nmax[:, u % UBUF, h:h + 1], accum_out=rsum[:, u % UBUF, h:h + 1])
                last.then_inc(s_exp, 1)

            def evac_probs(u, g, bank_of=None):
                q, j = u // TILES, u % TILES
                ps = psT if bank_of is None else bank_of
                act.wait_ge(s_trn, g * UNITS + u + 1)
                if q >= 2 and j == 0:
                    act.wait_ge(s_pv, g * HQ + q - 1)
                copy(probT[:, q % 2, :, j * P:(j + 1) * P],
                     ps[:, :].rearrange("p (h t) -> p h t", h=4)).then_inc(s_pt, 1)

            def evac_y(q, g):
                act.wait_ge(s_pv, g * HQ + q + 1)
                copy(yt_hl[:, 0, q], psT[:, :]).then_inc(s_yh, 1)

            def token_rows(j, g, ps=psS):
                act.wait_ge(s_tg, g * TILES + j + 1)
                if j >= 2:
                    act.wait_ge(s_h1, g * TILES + j - 1)
                copy(tokr[:, j % 2], ps[:, :], inv[:, TK:TK + 1]).then_inc(s_tokr, 1)

            def split_x(j, g, b):
                act.wait_ge(s_xt, g * TILES + j + 1)
                copy(xt_hl[:, 0, :, j * P:(j + 1) * P],
                     psU[b][:, :].rearrange("p (k t) -> p k t", k=KC)).then_inc(s_xh, 1)

            def square(i, g):
                act.wait_ge(s_up, g * IC + i + 1)
                nc.scalar.activation(relu[:, i % 2], psU[i % 2][:, :], ACT.Relu,
                                     scale=2.0 ** -(XSHIFT + RSHIFT)).then_inc(s_relu, 1)
                act.wait_ge(s_relu, g * IC + i + 1)
                if i >= 2:
                    act.wait_ge(s_sl, g * IC + i - 1)
                nc.scalar.activation(sqr[:, i % 2], relu[:, i % 2], ACT.Square).then_inc(s_sq, 1)
                act.wait_ge(s_sq, g * IC + i + 1)
                if i >= RING:
                    act.wait_ge(s_dn, g * (IC - 1) + i - RING + 1)
                copy(sq_hl[:, i % RING, 0], sqr[:, i % 2]).then_inc(s_sh, 1)

            def shared_norm(j, g):
                act.wait_ge(s_nb, g + 1)
                nc.scalar.activation(y[:, j], y[:, j], ACT.Identity, scale=rsy[:, j:j + 1],
                                     bias=nbias[:, j:j + 1]).then_inc(s_zn, 1)

            exps(0, 0)
            up_high(3)
            exps(1, 0)
            for u in range(UNITS):
                if u < UNITS - 2:
                    exps(u + 2, 0)
                if u == 4:
                    act.wait_ge(s_wlo, 3)
                if u % TILES == 0 and u > 0:
                    evac_y(u // TILES - 1, 0)
                evac_probs(u, 0, psU[u % 2])
                if u == 0:
                    output_high()
                if u == 1:
                    expert_high()
                if u in (5, 6, 7, 8):
                    down_squares(u - 5)
            evac_y(HQ - 1, 0)
            act.wait_ge(s_uplo, KC)
            for j in range(3):
                token_rows(j, 0, psY[j % 2])
            split_x(0, 0, 1)
            token_rows(3, 0, psY[1])
            split_x(1, 0, 1)
            split_x(2, 0, 1)
            split_x(3, 0, 0)
            act.wait_ge(s_dnlo, 4)
            with act.Fori(0, GROUPS - 1) as g:
                for i in range(IC):
                    square(i, g)
                    if i > TILES and i % TILES == 1:
                        evac_y(i // TILES - 1, g + 1)
                    exps(i, g + 1)
                    if i > 0:
                        evac_probs(i - 1, g + 1)
                evac_probs(UNITS - 1, g + 1)
                evac_y(HQ - 1, g + 1)
                for j in range(3):
                    token_rows(j, g + 1)
                split_x(0, g + 1, 1)
                token_rows(3, g + 1)
                split_x(1, g + 1, 1)
                split_x(2, g + 1, 1)
                split_x(3, g + 1, 0)
                for j in range(TILES):
                    shared_norm(j, g)
            for i in range(IC):
                square(i, GROUPS - 1)

        @block.vector
        def _(dve):
            chain = [0]

            def link(ins):
                chain[0] += 1
                ins.then_inc(s_dve, 1)
                dve.wait_ge(s_dve, chain[0])

            def largest(col, src, ax):
                return nc.vector.tensor_reduce(mx[:, col:col + 1], src, ax, ALU.max, apply_absolute_value=True)

            def wrap(ids_i, f, t):
                link(nc.vector.tensor_scalar(t, ids_i, 0.0, float(P), ALU.is_lt, ALU.mult))
                link(nc.vector.tensor_tensor(f, ids_i, t, ALU.add))
                link(nc.vector.tensor_scalar(f, f, float(P - 1), 0.0, ALU.min, ALU.max))

            def scales(a, b, n):
                dve.wait_ge(s_am, n)
                link(nc.vector.tensor_scalar(p2[:, a:b], am[:, a:b], 2.0 ** -100, 2.0 ** 100, ALU.max, ALU.min))
                link(nc.vector.tensor_scalar(p2[:, a:b].bitcast(I32), p2[:, a:b].bitcast(I32), 0x7F800000, None,
                                             ALU.bitwise_and))
                link(nc.vector.tensor_scalar(inv[:, a:b], p2[:, a:b], 2.0 ** -TOP, None, ALU.mult))
                link(nc.vector.tensor_scalar(scl[:, a:b].bitcast(I32), p2[:, a:b].bitcast(I32), 0x7F800000, None,
                                             ALU.bitwise_xor))
                link(nc.vector.tensor_scalar(scl[:, a:b], scl[:, a:b], 2.0 ** (TOP - 1), None, ALU.mult))
                nc.vector.tensor_scalar(p2[:, a:b], scl[:, a:b], 1.0, None, ALU.mult).then_inc(s_scl, 1)

            def low(dst, src, high, col, s_high, s_low, n):
                dve.wait_ge(s_high, n)
                nc.vector.scalar_tensor_tensor(dst, src, scl[:, col:col + 1], high, ALU.mult,
                                               ALU.subtract).then_inc(s_low, 1)

            dve.wait_ge(s_iota, 1)
            link(nc.vector.tensor_copy(iota_v, iota_vi))
            dve.wait_ge(ld["idc"], 16)
            wrap(idc[:, :].bitcast(I32), tmpc2[:, :], tmpc[:, :])
            dve.wait_ge(ld["emb"], 16)
            link(nc.vector.tensor_tensor_reduce(out=tok[:, :], in0=row, in1=row, scale=1.0, scalar=0.0, op0=ALU.mult,
                                                op1=ALU.add, accum_out=stat[:, 0, 3:4]))
            nc.vector.tensor_scalar(stat[:, 0, 0:1], stat[:, 0, 3:4], 1.0 / DM, EPS_RMS, ALU.mult,
                                    ALU.add).then_inc(s_var0, 1)
            dve.wait_ge(ld["nw"], 16)
            dve.wait_ge(s_rs0, 1)
            nc.vector.scalar_tensor_tensor(row, row, stat[:, 1, 0:1], nrm, ALU.mult, ALU.mult).then_inc(s_row, 1)
            nc.vector.tensor_tensor(ohr, iota_v.unsqueeze(1).broadcast_to([P, SEQ // P, P]),
                                    tmpc2[:, :].unsqueeze(2).broadcast_to([P, SEQ // P, P]), ALU.is_equal).then_inc(s_ohr, 1)
            dve.wait_ge(s_psb, 1)
            link(nc.vector.tensor_tensor_reduce(out=nrm, in0=tok[:, :], in1=tok[:, :], scale=1.0, scalar=0.0,
                                                op0=ALU.mult, op1=ALU.add, accum_out=stat[:, 0, 3:4]))
            nc.vector.tensor_scalar(stat[:, 0, 1:2], stat[:, 0, 3:4], 1.0 / DM, EPS_RMS, ALU.mult,
                                    ALU.add).then_inc(s_var0, 1)
            dve.wait_ge(s_rs0, 2)
            link(nc.vector.tensor_scalar(tok[:, :], tok[:, :], stat[:, 1, 1:2], None, ALU.mult))
            link(nc.vector.bn_stats(bn0[:, :], tok[:, :]))
            link(nc.vector.bn_aggr(stat[:, 0, 4:6], bn0[:, :]))
            nc.vector.tensor_scalar(stat[:, 0, 2:3], stat[:, 0, 5:6], EPS_LN, None, ALU.add).then_inc(s_var0, 1)
            dve.wait_ge(s_rs0, 3)
            nc.vector.tensor_scalar(row, tok[:, :], stat[:, 0, 4:5], stat[:, 1, 2:3], ALU.subtract,
                                    ALU.mult).then_inc(s_row, 1)
            dve.wait_ge(ld["bo"], 16)
            dve.wait_ge(s_row, 2)
            link(nc.vector.tensor_tensor(tok[:, :], tok[:, :], bo_sb, ALU.add))
            link(largest(TK, tok[:, :], AX.X))

            def counts_done(b):
                lb = lnc[:, 4 * b:4 * b + 4, :].rearrange("p j v -> p (j v)")
                dve.wait_ge(s_unseen, b + 1)
                nc.vector.tensor_tensor(lb, lb, unseen, ALU.subtract).then_inc(s_lnc, 1)

            counts_done(0)
            counts_done(1)
            for k in range(KC):
                dve.wait_ge(ld[f"up{k}"], 16)
                link(nc.vector.tensor_reduce(mxs[:, k:k + 1], rawu[:, k * INTER:(k + 1) * INTER], AX.X, ALU.max,
                                             apply_absolute_value=True))
            largest(UP, mxs[:, :], AX.X).then_inc(s_mx, 1)
            dve.wait_ge(s_mx, 1)
            dve.wait_ge(ld["bqk"], 32)
            dve.wait_ge(s_qkv, 1)
            for m in range(KC):
                last = nc.vector.tensor_scalar(qT[:, m], psU[0][:, m * P:(m + 1) * P], bqk[:, 0, m:m + 1], float(HD) ** -0.5,
                                               ALU.add, ALU.mult)
            last.then_inc(s_qk, 1)
            dve.wait_ge(s_qkv, 2)
            for m in range(KC):
                last = nc.vector.tensor_scalar(kT[:, m], psU[1][:, m * P:(m + 1) * P], bqk[:, 1, m:m + 1], None, ALU.add)
            last.then_inc(s_qk, 1)
            scales(UP, UP + 1, 1)
            dve.wait_ge(s_qkv, 3)
            dve.wait_ge(ld["bv"], 16)
            nc.vector.tensor_tensor(val[:, :], psT[:, :], bv_sb, ALU.add).then_inc(s_vsum, 1)
            dve.wait_ge(s_vsum, 1)
            link(largest(VL, val[:, :], AX.X))
            dve.wait_ge(s_tab, 1)
            for j in range(4):
                link(nc.vector.tensor_reduce(mxs[:, j:j + 1], bank[j][:, :], AX.X, ALU.max, apply_absolute_value=True))
            largest(SC, mxs[:, :], AX.X).then_inc(s_mx, 1)
            dve.wait_ge(ld["gate"], 16)
            largest(GA, rawg[:, :, :], AX.XY).then_inc(s_mx, 1)
            scales(SC, VL + 1, 2)
            nc.vector.tensor_scalar(val[:, :], val[:, :], scl[:, VL:VL + 1], None, ALU.mult).then_inc(s_val, 1)
            for j in range(4):
                low(sc_hl[:, 1].rearrange("p (c j) v -> p c j v", j=4)[:, :, j, :],
                    bank[j][:, :].rearrange("p (c v) -> p c v", v=P),
                    sc_hl[:, 0].rearrange("p (c j) v -> p c j v", j=4)[:, :, j, :], SC, s_hi, s_lo, j + 1)
            low(tk_hl[:, 1], tok[:, :], tk_hl[:, 0], TK, s_hi, s_lo, 5)
            counts_done(2)
            counts_done(3)
            def output_low():
                low(wo_hl[:, 1], raww, wo_hl[:, 0], WO, s_whi, s_wlo, 1)

            def expert_low():
                low(ex_hl[:, 1], rawe, ex_hl[:, 0], EX, s_whi, s_wlo, 2)
                low(gt_hl[:, 1], rawg[:, :, :], gt_hl[:, 0], GA, s_whi, s_wlo, 3)

            def undo_factors():
                link(nc.vector.tensor_scalar(kap[:, KO:KO + 1], inv[:, VL:VL + 1], inv[:, WO:WO + 1], None, ALU.mult))
                link(nc.vector.tensor_scalar(kap[:, KE:KE + 1], inv[:, GA:GA + 1], inv[:, EX:EX + 1],
                                             2.0 ** (-2 * XSHIFT), ALU.mult, ALU.mult))
                link(nc.vector.tensor_scalar(kap[:, KY:KY + 1], inv[:, UP:UP + 1], 2.0 ** RSHIFT, None, ALU.mult))
                link(nc.vector.tensor_scalar(kap[:, KY:KY + 1], kap[:, KY:KY + 1], kap[:, KY:KY + 1], inv[:, DN:DN + 1],
                                             ALU.mult, ALU.mult))

            def down_high(k):
                raw = rawd[:, k * 2048:(k + 1) * 2048].rearrange("p (k n) -> p k n", k=4)
                nc.vector.tensor_scalar(dn_hl[:, 0, 4 * k:4 * k + 4], raw, scl[:, DN:DN + 1], None, ALU.mult)
                nc.vector.tensor_scalar(raw, raw, scl[:, DN:DN + 1], None, ALU.mult).then_inc(s_dnhi, 1)

            def carry_wait():
                nc.vector.tensor_copy(carrier[:, :], half[:, 0:1])

            def bias_and_max(u, g, ps=psS):
                tile = g * TILES + u % TILES
                dve.wait_ge(s_scored, g * UNITS + u + 1)
                need(dve, s_trn, g * UNITS + u + 1 - UBUF)
                nc.vector.scalar_tensor_tensor(
                    prob[:, u % UBUF], ps[:, :].rearrange("p (h v) -> p h v", h=4), inv[:, SC:SC + 1],
                    lnc[:, bass.ds(tile, 1), :].broadcast_to([P, 4, P]), ALU.mult, ALU.add).then_inc(s_added, 1)
                dve.wait_ge(s_added, g * UNITS + u + 1)
                nc.vector.tensor_reduce(nmax[:, u % UBUF], prob[:, u % UBUF], AX.X, ALU.max, negate=True).then_inc(s_max, 1)

            def normalise(u, g):
                dve.wait_ge(s_exp, g * UNITS + u + 1)
                nc.vector.reciprocal(rinv[:, u % UBUF], rsum[:, u % UBUF]).then_inc(s_rec, 1)
                dve.wait_ge(s_rec, g * UNITS + u + 1)
                nc.vector.tensor_tensor(prob[:, u % UBUF], prob[:, u % UBUF],
                                        rinv[:, u % UBUF].unsqueeze(2).broadcast_to([P, 4, P]), ALU.mult).then_inc(s_norm, 1)

            def low_y(q, g):
                dve.wait_ge(s_yh, g * HQ + q + 1)
                nc.vector.tensor_tensor(yt_hl[:, 1, q], psT[:, :], yt_hl[:, 0, q], ALU.subtract).then_inc(s_yl, 1)

            def residual(j, g, ps=psT):
                dve.wait_ge(s_wo, g * TILES + j + 1)
                dve.wait_ge(s_tokr, g * TILES + j + 1)
                need(dve, s_h1b, g * TILES)
                nc.vector.scalar_tensor_tensor(h1[:, j], ps[:, :], kap[:, KO:KO + 1], tokr[:, j % 2], ALU.mult,
                                               ALU.add).then_inc(s_h1, 1)
                dve.wait_ge(s_h1, g * TILES + j + 1)
                nc.vector.bn_stats(bnx[:, j], h1[:, j]).then_inc(s_bn, 1)
                dve.wait_ge(s_bn, g * TILES + j + 1)
                carry_wait()
                nc.vector.bn_aggr(mvx[:, j], bnx[:, j]).then_inc(s_agg, 1)
                dve.wait_ge(s_agg, g * TILES + j + 1)
                nc.vector.tensor_scalar(vex[:, j:j + 1], mvx[:, j, 1:2], EPS_LN, 2.0 ** (-2 * XSHIFT), ALU.add,
                                        ALU.mult).then_inc(s_ve, 1)

            def layer_norm(j, g):
                dve.wait_ge(s_rs, g * TILES + j + 1)
                if j >= 2:
                    dve.wait_ge(s_xt, g * TILES + j - 1)
                nc.vector.tensor_scalar(xrow[:, j % 2], h1[:, j], mvx[:, j, 0:1], rsx[:, j:j + 1], ALU.subtract,
                                        ALU.mult).then_inc(s_x, 1)

            def low_x(j, g, b):
                dve.wait_ge(s_xh, g * TILES + j + 1)
                c = slice(j * P, (j + 1) * P)
                nc.vector.tensor_tensor(xt_hl[:, 1, :, c], psU[b][:, :].rearrange("p (k t) -> p k t", k=KC),
                                        xt_hl[:, 0, :, c], ALU.subtract).then_inc(s_xl, 1)

            def routing(g):
                dve.wait_ge(s_gate, g + 1)
                carry_wait()
                for j in range(TILES):
                    last = nc.vector.max(top8[:, j], psS[:, j * NEXP:(j + 1) * NEXP])
                last.then_inc(s_top, 1)
                dve.wait_ge(s_top, g + 1)
                for j in range(TILES):
                    last = nc.vector.tensor_scalar(rout[:, j:j + 1], top8[:, j, 0:1], top8[:, j, 1:2], kap[:, KE:KE + 1],
                                                   ALU.add, ALU.mult)
                last.then_inc(s_rout, 1)

            def low_square(i, g):
                dve.wait_ge(s_sh, g * IC + i + 1)
                nc.vector.tensor_tensor(sq_hl[:, i % RING, 1], sqr[:, i % 2], sq_hl[:, i % RING, 0],
                                        ALU.subtract).then_inc(s_sl, 1)

            def expert_rows(j, g, ps=None):
                if j == 0:
                    dve.wait_ge(s_rout, g + 1)
                dve.wait_ge(s_h1b, g * TILES + j + 1)
                dve.wait_ge(s_ex, g * TILES + j + 1)
                nc.vector.tensor_scalar(y[:, j], (ps or psU[EXPERT_BANK[j]])[:, :], rout[:, j:j + 1], None, ALU.mult).then_inc(s_moe, 1)

            def shared_rows(j, g):
                dve.wait_ge(s_dt, g * TILES + j + 1)
                dve.wait_ge(s_moe, g * TILES + j + 1)
                nc.vector.scalar_tensor_tensor(y[:, j], psY[j][:, :], kap[:, KY:KY + 1], y[:, j], ALU.mult,
                                               ALU.add).then_inc(s_yev, 1)
                dve.wait_ge(s_yev, g * TILES + j + 1)
                nc.vector.bn_stats(bny[:, j], y[:, j]).then_inc(s_bny, 1)

            def shared_norm(g):
                dve.wait_ge(s_bny, (g + 1) * TILES)
                carry_wait()
                for j in range(TILES):
                    last = nc.vector.bn_aggr(mvy[:, j], bny[:, j])
                last.then_inc(s_aggy, 1)
                dve.wait_ge(s_aggy, g + 1)
                nc.vector.tensor_scalar(nmean[:, :], mvy[:, :, 0], -1.0, None, ALU.mult)
                nc.vector.tensor_scalar(vey[:, :], mvy[:, :, 1], EPS_LN, None, ALU.add).then_inc(s_vey, 1)

            def last_rows(j, g):
                shared_rows(j, g)
                dve.wait_ge(s_bny, g * TILES + j + 1)
                link(nc.vector.bn_aggr(mvy[:, j], bny[:, j]))
                nc.vector.tensor_scalar(vey[:, j:j + 1], mvy[:, j, 1:2], EPS_LN, None, ALU.add).then_inc(s_vey, 1)
                link(nc.vector.scalar_tensor_tensor(y[:, j], y[:, j], mvy[:, j, 0:1], gam, ALU.subtract, ALU.mult))
                dve.wait_ge(s_rsy, g + j + 1)
                dve.wait_ge(s_h1b, g * TILES + j + 1)
                dve.wait_ge(s_out[j % 2], g * (8 * TILES) + (j // 2 + 1) * 16)
                nc.vector.scalar_tensor_tensor(fin[:, j % 2], y[:, j], rsy[:, j:j + 1], h1b[:, j], ALU.mult,
                                               ALU.add).then_inc(s_fin, 1)

            for u in range(3):
                bias_and_max(u, 0, psY[u])
            for u in range(UNITS):
                normalise(u, 0)
                if u < UNITS - 3:
                    bias_and_max(u + 3, 0, psY[(u + 3) % 4])
                if u % TILES == 0 and u > 0:
                    low_y(u // TILES - 1, 0)
                if u == 0:
                    scales(WO, GA + 1, 3)
                if u == 2:
                    output_low()
                if u == 3:
                    expert_low()
                if u == 11:
                    scales(DN, DN + 1, 4)
                if u in (11, 12, 13, 14):
                    down_high(u - 11)
            low_y(HQ - 1, 0)
            undo_factors()
            dve.wait_ge(s_uplo, KC)
            residual(0, 0, psY[2])
            residual(1, 0, psY[3])
            layer_norm(0, 0)
            residual(2, 0, psY[2])
            low_x(0, 0, 1)
            layer_norm(1, 0)
            residual(3, 0, psY[3])
            low_x(1, 0, 1)
            layer_norm(2, 0)
            layer_norm(3, 0)
            low_x(2, 0, 1)
            low_x(3, 0, 0)
            with dve.Fori(0, GROUPS - 1) as g:
                routing(g)
                for i in range(IC):
                    if i > 0:
                        normalise(i - 1, g + 1)
                    bias_and_max(i, g + 1)
                    if i > TILES and i % TILES == 1:
                        low_y(i // TILES - 1, g + 1)
                    low_square(i, g)
                normalise(UNITS - 1, g + 1)
                expert_rows(0, g)
                expert_rows(1, g)
                low_y(HQ - 1, g + 1)
                expert_rows(2, g)
                residual(0, g + 1)
                shared_rows(0, g)
                residual(1, g + 1)
                layer_norm(0, g + 1)
                shared_rows(1, g)
                residual(2, g + 1)
                low_x(0, g + 1, 1)
                layer_norm(1, g + 1)
                shared_rows(2, g)
                residual(3, g + 1)
                low_x(1, g + 1, 1)
                layer_norm(2, g + 1)
                layer_norm(3, g + 1)
                expert_rows(3, g)
                low_x(2, g + 1, 1)
                shared_rows(3, g)
                low_x(3, g + 1, 0)
                shared_norm(g)
            routing(GROUPS - 1)
            for i in range(IC):
                low_square(i, GROUPS - 1)
                if i < TILES:
                    expert_rows(i, GROUPS - 1, psT)
            for j in range(TILES):
                last_rows(j, GROUPS - 1)

        @block.tensor
        def _(pe):
            mm = nc.tensor.matmul

            def split_product(dst, stat_hl, mov_hl, n, steps, start=True, stop=True):
                for k in range(steps):
                    for a, b in ((0, 0), (0, 1), (1, 0)):
                        last = mm(dst, stat_hl(a, k), mov_hl(b, k), start=start and k == 0 and a == b,
                                  stop=stop and k == steps - 1 and a == 1)
                return last

            def counts(b, dst):
                for j in range(4 * b, 4 * b + 4):
                    c = slice((j % 4) * P, (j % 4 + 1) * P)
                    for i in range(j):
                        mm(dst[:, c], ones[:, :], ohr[:, i, :], start=i == 0, stop=False)
                    last = mm(dst[:, c], tri[:, :], ohr[:, j, :], start=j == 0, stop=True)
                last.then_inc(s_cnt, 1)

            def token_columns(n):
                pe.wait_ge(s_row, n + 1)
                for k in range(KC):
                    last = nc.tensor.transpose(psS[:, k * P:(k + 1) * P], row[:, k * P:(k + 1) * P], ident[:, :])
                last.then_inc(s_rowT, 1)

            pe.wait_ge(s_pool0, 10)
            token_columns(0)
            pe.wait_ge(ld["proj"], 16)
            pe.wait_ge(s_colT, 1)
            for k in range(KC):
                last = mm(psT[:, :], colT[:, k], pj_sb[:, k], start=k == 0, stop=k == KC - 1)
            last.then_inc(s_proj, 1)
            pe.wait_ge(s_ohr, 1)
            counts(0, bank[0])
            counts(1, bank[1])
            for j in range(SEQ // P):
                c = slice((j % 8) * P, (j % 8 + 1) * P)
                last = nc.tensor.transpose(psU[j // 8][:, :].bitcast(F16)[:, c], ohr[:, j, :], identh)
                if j % 8 == 7:
                    last.then_inc(s_ohT, 1)
            token_columns(1)
            pe.wait_ge(s_colT, 2)
            pe.wait_ge(s_oht, 2)
            for i, w in enumerate((wq_sb, wk_sb)):
                pe.wait_ge(ld["wq" if i == 0 else "wk"], 16)
                for m in range(KC):
                    for k in range(KC):
                        last = mm(psU[i][:, m * P:(m + 1) * P], w[:, k, m * P:(m + 1) * P], colT[:, k],
                                  start=k == 0, stop=k == KC - 1)
                last.then_inc(s_qkv, 1)
            pe.wait_ge(ld["wv"], 16)
            for k in range(KC):
                last = mm(psT[:, :], colT[:, k], wv_sb[:, k], start=k == 0, stop=k == KC - 1)
            last.then_inc(s_qkv, 1)
            pe.wait_ge(s_qk, 2)
            pe.wait_ge(s_unseen, 2)
            for c in range(KC):
                for j in range(4):
                    r = slice(HD * j, HD * (j + 1))
                    last = mm(bank[j][:, c * P:(c + 1) * P], qT[r, c, :], kT[r, c, :], start=True, stop=True)
            last.then_inc(s_tab, 1)
            counts(2, psS)
            pe.wait_ge(s_vsum, 1)
            counts(3, psT)

            def score(u, g, ps=psS, banks=1):
                q, j = u // TILES, u % TILES
                need(pe, s_added, g * UNITS + u + 1 - banks)
                if u == 0:
                    need(pe, s_tokr, g * TILES)
                t = bass.ds(g * GT + j * P, P)
                for a in range(2):
                    last = mm(ps[:, :], oht[:, t], sc_hl[:, a, 4 * q:4 * q + 4, :].rearrange("p h v -> p (h v)"),
                              start=a == 0, stop=a == 1)
                last.then_inc(s_scored, 1)

            def transpose_probs(u, g, alone=False):
                ps = psU[u % 2] if alone else psT
                pe.wait_ge(s_norm, g * UNITS + u + 1)
                if alone:
                    need(pe, s_pt, u - 1)
                else:
                    need(pe, s_pt, g * UNITS + u)
                    if u % TILES == 0 and u > 0:
                        pe.wait_ge(s_yl, g * HQ + u // TILES)
                    if u == 0:
                        need(pe, s_h1, g * TILES)
                for h in range(4):
                    last = nc.tensor.transpose(ps[:, h * P:(h + 1) * P], prob[:, u % UBUF, h, :], ident[:, :])
                last.then_inc(s_trn, 1)

            def attend(q, g, alone=False):
                pe.wait_ge(s_pt, g * UNITS + (q + 1) * TILES)
                if alone:
                    need(pe, s_yl, q)
                for h in range(4):
                    c = (4 * q + h) * HD
                    last = mm(psT[HD * h:HD * (h + 1), :], val[:, c:c + HD], probT[:, q % 2, h, :],
                              start=True, stop=True)
                last.then_inc(s_pv, 1)

            def attention_out(j, g, alone=False):
                psK, psO = (psY[j % 2], psY[2 + j % 2]) if alone else (psS, psT)
                if alone:
                    pe.wait_ge(s_yl, HQ)
                    need(pe, s_h1, j - 1)
                elif j == 0:
                    pe.wait_ge(s_yl, (g + 1) * HQ)
                    pe.wait_ge(s_added, (g + 1) * UNITS)
                else:
                    pe.wait_ge(s_tokr, g * TILES + j)
                    pe.wait_ge(s_h1, g * TILES + j)
                t = bass.ds(g * GT + j * P, P)
                for a in range(2):
                    last = mm(psK[:, :], oht[:, t], tk_hl[:, a], start=a == 0, stop=a == 1)
                last.then_inc(s_tg, 1)
                c = slice(j * P, (j + 1) * P)
                split_product(psO[:, :], lambda a, k: yt_hl[:, a, k, c], lambda b, k: wo_hl[:, b, k], DM,
                              KC).then_inc(s_wo, 1)

            def transpose_rows(j, g, b, bank_free):
                pe.wait_ge(s_x, g * TILES + j + 1)
                if bank_free is not None:
                    need(pe, *bank_free)
                for k in range(KC):
                    last = nc.tensor.transpose(psU[b][:, k * P:(k + 1) * P], xrow[:, j % 2, k * P:(k + 1) * P],
                                               ident[:, :])
                last.then_inc(s_xt, 1)

            def gate_logits(g):
                pe.wait_ge(s_tokr, (g + 1) * TILES)
                for j in range(TILES):
                    pe.wait_ge(s_xl, g * TILES + j + 1)
                    c = slice(j * P, (j + 1) * P)
                    last = split_product(psS[:, j * NEXP:(j + 1) * NEXP], lambda a, k: xt_hl[:, a, k, c],
                                         lambda b, k: gt_hl[:, b, k, :], NEXP, KC)
                last.then_inc(s_gate, 1)

            def up_chunk(i, g):
                if i >= 2:
                    pe.wait_ge(s_relu, g * IC + i - 1)
                c = slice(i * P, (i + 1) * P)
                split_product(psU[i % 2][:, :], lambda a, k: up_hl[:, a, k, c], lambda b, k: xt_hl[:, b, k, :], GT,
                              KC).then_inc(s_up, 1)

            def down_tile(j, i, g):
                c = slice(j * P, (j + 1) * P)
                return split_product(psY[j][:, :], lambda a, k: sq_hl[:, i % RING, a, c],
                                     lambda b, k: dn_hl[:, b, i], DM, 1, start=i == 0, stop=i == IC - 1)

            def down_chunk(i, g):
                pe.wait_ge(s_sl, g * IC + i + 1)
                for j in range(TILES):
                    last = down_tile(j, i, g)
                last.then_inc(s_dn, 1)

            def expert_product(j, g, ps=None):
                if ps is not None:
                    pe.wait_ge(s_moe, g * TILES + j)
                elif j < 2:
                    pe.wait_ge(s_relu, g * IC + IC - 1 + j)
                else:
                    pe.wait_ge(s_moe, g * TILES + 2 * j - 3)
                c = slice(j * P, (j + 1) * P)
                split_product((ps or psU[EXPERT_BANK[j]])[:, :], lambda a, k: xt_hl[:, a, k, c], lambda b, k: ex_hl[:, b, k], DM,
                              KC).then_inc(s_ex, 1)

            pe.wait_ge(s_lo, 5)
            pe.wait_ge(s_val, 1)
            for u in range(3):
                score(u, 0, psY[u], 4)
            for u in range(UNITS):
                if u < UNITS - 3:
                    score(u + 3, 0, psY[(u + 3) % 4], 4)
                if u == 2:
                    pe.wait_ge(s_unseen, 4)
                transpose_probs(u, 0, True)
                if u % TILES == 0 and u > 0:
                    attend(u // TILES - 1, 0, True)
            attend(HQ - 1, 0, True)
            pe.wait_ge(s_wlo, 3)
            for j in range(3):
                attention_out(j, 0, True)
            transpose_rows(0, 0, 1, None)
            attention_out(3, 0, True)
            transpose_rows(1, 0, 1, (s_xl, 1))
            transpose_rows(2, 0, 1, (s_xl, 2))
            transpose_rows(3, 0, 0, None)
            pe.wait_ge(s_uplo, KC)
            pe.wait_ge(s_dnlo, 4)
            with pe.Fori(0, GROUPS - 1) as g:
                gate_logits(g)
                for i in range(IC):
                    up_chunk(i, g)
                    if i > TILES and i % TILES == 1:
                        attend(i // TILES - 1, g + 1)
                    if i == 0:
                        pe.wait_ge(s_rout, g + 1)
                    score(i, g + 1)
                    if i > 0:
                        down_chunk(i - 1, g)
                        transpose_probs(i - 1, g + 1)
                expert_product(0, g)
                transpose_probs(UNITS - 1, g + 1)
                expert_product(1, g)
                attend(HQ - 1, g + 1)
                expert_product(2, g)
                attention_out(0, g + 1)
                pe.wait_ge(s_sl, g * IC + IC)
                down_tile(0, IC - 1, g).then_inc(s_dt, 1)
                attention_out(1, g + 1)
                down_tile(1, IC - 1, g).then_inc(s_dt, 1)
                attention_out(2, g + 1)
                transpose_rows(0, g + 1, 1, (s_moe, g * TILES + 2))
                down_tile(2, IC - 1, g).then_inc(s_dt, 1)
                attention_out(3, g + 1)
                transpose_rows(1, g + 1, 1, (s_xl, g * TILES + TILES + 1))
                expert_product(3, g)
                transpose_rows(2, g + 1, 1, (s_xl, g * TILES + TILES + 2))
                down_tile(3, IC - 1, g).then_inc(s_dt, 1)
                transpose_rows(3, g + 1, 0, (s_moe, g * TILES + 4))
            gate_logits(GROUPS - 1)
            for i in range(IC):
                up_chunk(i, GROUPS - 1)
                if i == 0:
                    pe.wait_ge(s_rout, GROUPS)
                if i > 0:
                    down_chunk(i - 1, GROUPS - 1)
                if i < TILES:
                    expert_product(i, GROUPS - 1, psT)
            pe.wait_ge(s_sl, GROUPS * IC)
            for j in range(TILES):
                down_tile(j, IC - 1, GROUPS - 1).then_inc(s_dt, 1)


def kernel(x, L0_tok_emb_table, L0_tok_norm_weight, L0_tok_proj_weight, L0_attn_Wq, L0_attn_bq, L0_attn_Wk,
           L0_attn_bk, L0_attn_Wv, L0_attn_bv, L0_attn_Wo, L0_attn_bo, L0_ffn_gate_w, L0_ffn_up_w, L0_ffn_down_w,
           L0_ffn_expert_weight, L0_ffn_ln_gamma, L0_ffn_ln_beta):
    import numpy as np
    import concourse.bacc as bacc
    from concourse.bass_utils import run_bass_kernel_spmd

    def heads_last(w):
        return np.asarray(w).transpose(1, 0, 2).reshape(DM, DM)

    def column(b):
        return np.asarray(b).reshape(KC, P).T

    given = {
        "ids_col": np.asarray(x).reshape(SEQ // P, P).T, "emb": L0_tok_emb_table, "norm_w": L0_tok_norm_weight,
        "proj_t": np.asarray(L0_tok_proj_weight).T, "wq": heads_last(L0_attn_Wq), "wk": heads_last(L0_attn_Wk),
        "wv": heads_last(L0_attn_Wv), "bq": column(L0_attn_bq), "bk": column(L0_attn_bk),
        "bv": np.asarray(L0_attn_bv).reshape(DM), "wo": L0_attn_Wo, "bo": L0_attn_bo, "up": L0_ffn_up_w,
        "down": L0_ffn_down_w, "expert": L0_ffn_expert_weight, "gate": L0_ffn_gate_w, "gamma": L0_ffn_ln_gamma,
        "beta": L0_ffn_ln_beta,
    }
    nc = bacc.Bacc("TRN2", target_bir_lowering=False, num_devices=1)
    arrays, aps = {}, {}
    for name, a in given.items():
        a = np.ascontiguousarray(a)
        arrays[f"in_{name}"] = a
        aps[name] = nc.dram_tensor(f"in_{name}", a.shape, mybir.dt.from_np(a.dtype), kind="ExternalInput").ap()
    out = nc.dram_tensor("out_rows", (SEQ, DM), F32, kind="ExternalOutput").ap()
    tower(nc, out=out, **aps)
    got = run_bass_kernel_spmd(nc, [arrays], core_ids=[0]).results[0]["out_rows"]
    return got.reshape(1, SEQ, DM)
```

```python
import concourse.bass as bass
from concourse import mybir
from contextlib import ExitStack

F32 = mybir.dt.float32
F16 = mybir.dt.float16
BF16 = mybir.dt.bfloat16
I32 = mybir.dt.int32
ALU = mybir.AluOpType
ACT = mybir.ActivationFunctionType
AX = mybir.AxisListType
ABSMAX = bass.bass_isa.ReduceOp.absmax

P = 128
SEQ = 2048
DM = 512
KC = DM // P
HEADS = 16
HD = DM // HEADS
INTER = 2048
IC = INTER // P
NEXP = 8
GT = 512
GROUPS = SEQ // GT
TILES = GT // P
HQ = HEADS // 4
UNITS = HQ * TILES
UBUF = 4
RING = 3

EXPERT_BANK = (0, 1, 0, 0)
TOP = 14
XSHIFT = 11
RSHIFT = 17
UP_SCALED = 1
WARM_UP = 10
KEEP_BUSY = 10
DN_UNITS = (6, 7, 9, 10)
RAW_UNIT = 12
EXPERT_UNIT = 13
VAL_UNIT = 3
TINY = 1e-18
UNSEEN = 1e28
EPS_RMS = 1e-6
EPS_LN = 1e-5


def tower(nc, ids_col, emb, norm_w, proj_t, wq, wk, wv, bq, bk, bv, wo, bo, up, down, expert, gate, gamma, beta, out):
    ctx = ExitStack()
    with ctx:
        def sb(name, shape, dt):
            return ctx.enter_context(nc.sbuf_tensor(name, shape, dt))

        def sem(name):
            return ctx.enter_context(nc.semaphore(name))

        wo_hl = sb("wo_hl", [P, 2, KC, DM], F16)
        up_hl = sb("up_hl", [P, 2, KC, INTER], F16)
        ex_hl = sb("ex_hl", [P, 2, KC, DM], F16)
        dn_hl = sb("dn_hl", [P, 2, IC, DM], F16)
        gt_hl = sb("gt_hl", [P, 2, KC, NEXP], F16)
        sc_hl = sb("sc_hl", [P, 2, HEADS, P], F16)
        tk_hl = sb("tk_hl", [P, 2, DM], F16)
        oht = sb("oht", [P, SEQ], F16)
        lnc = sb("lnc", [P, SEQ // P, P], F32)
        val = sb("val", [P, DM], F32)
        prob = sb("prob", [P, UBUF, 4, P], F32)
        probT = sb("probT", [P, 2, 4, GT], F32)
        yt_hl = sb("yt_hl", [P, 2, HQ, GT], F16)
        rawu = sb("rawu", [P, KC * INTER], F32)
        tokr = rawu[:, 0:1024].rearrange("p (b n) -> p b n", b=2)
        xrow = rawu[:, 1024:2048].rearrange("p (b n) -> p b n", b=2)
        h1 = rawu[:, 2048:4096].rearrange("p (j n) -> p j n", j=TILES)
        h1b = rawu[:, 4096:6144].rearrange("p (j n) -> p j n", j=TILES)
        xt_hl = rawu[:, 6144:8192].bitcast(F16).rearrange("p (a k t) -> p a k t", a=2, k=KC)
        rawd = sb("rawd", [P, IC * DM], F32)
        relu = rawd[:, 0:1024].rearrange("p (b n) -> p b n", b=2)
        sqr = rawd[:, 1024:2048].rearrange("p (b n) -> p b n", b=2)
        y = rawd[:, 2048:4096].rearrange("p (j n) -> p j n", j=TILES)
        fin = rawd[:, 4096:5120].rearrange("p (b n) -> p b n", b=2)
        sq_hl = rawd[:, 5120:5120 + RING * DM].bitcast(F16).rearrange("p (b a n) -> p b a n", b=RING, a=2)
        gam = rawd[:, 5120 + RING * DM:5120 + RING * DM + DM]
        bet = rawd[:, 5120 + RING * DM + DM:5120 + RING * DM + 2 * DM]
        raww = yt_hl[:, :, :, :].rearrange("p a k n -> p (a k n)").bitcast(F32).rearrange("p (k n) -> p k n", k=KC)
        rawe = probT[:, 1]
        probT0 = probT[:, 0].rearrange("p h t -> p (h t)").rearrange("p (b h t) -> p b h t", b=UBUF, h=4)
        wflat = dn_hl[:, :, :, :].rearrange("p a k n -> p (a k n)").bitcast(F32).rearrange("p (w k n) -> p w k n", w=4, k=KC)
        pj_sb, wq_sb, wk_sb, wv_sb = (wflat[:, i] for i in range(4))
        exf = ex_hl[:, :, :, :].rearrange("p a k n -> p (a k n)")
        ohr = exf[:, 0:2048].rearrange("p (j v) -> p j v", v=P)
        ohr_sum = exf[:, 2048:3072].rearrange("p (b n) -> p b n", b=2)
        bv_sb = exf[:, 3072:4096].bitcast(F32)
        unseen = probT[:, 0]
        pflat = prob[:, :, :, :].rearrange("p b j v -> p (b j v)")
        row = pflat[:, 0:DM]
        nrm = pflat[:, DM:2 * DM]
        colT = pflat[:, 2 * DM:3 * DM].rearrange("p (k v) -> p k v", k=KC)
        kT = pflat[:, 3 * DM:4 * DM].rearrange("p (k v) -> p k v", k=KC)
        tok = sb("tok", [P, DM], F32)
        sflat = sc_hl[:, :, :, :].rearrange("p a h v -> p (a h v)").bitcast(F32)
        bo_sb = sflat[:, 0:DM]
        qT = sflat[:, 2 * DM:3 * DM].rearrange("p (k v) -> p k v", k=KC)
        iota_v = sflat[:, 3 * DM:3 * DM + P]
        iota_vi = sflat[:, 3 * DM + P:3 * DM + 2 * P].bitcast(I32)
        identh = sflat[:, 3 * DM + 2 * P:3 * DM + 2 * P + P // 2].bitcast(F16)
        scrap = up_hl[:, 1, KC - 1].bitcast(F32).rearrange("p (b c v) -> p b c v", b=2, c=KC)
        ident = sb("ident", [P, P], F32)
        tri = sb("tri", [P, P], F16)
        ones = sb("ones", [P, P], F16)
        lnb = sb("lnb", [P, 2], F32)
        idc = sb("idc", [P, SEQ // P], F32)
        tmpc2 = sb("tmpc2", [P, SEQ // P], F32)
        tmpc = sb("tmpc", [P, SEQ // P], F32)
        bqk = sb("bqk", [P, 2, KC], F32)
        rawg = sb("rawg", [P, KC, NEXP], F32)
        mxs = sb("mxs", [P, 4], F32)
        ams = sb("ams", [P, 1], F32)
        mx = sb("mx", [P, 8], F32)
        am = sb("am", [P, 8], F32)
        p2 = sb("p2", [P, 8], F32)
        inv = sb("inv", [P, 8], F32)
        scl = sb("scl", [P, 8], F32)
        kap = sb("kap", [P, 4], F32)
        stat = sb("stat", [P, 2, 8], F32)
        bn0 = sb("bn0", [P, 6], F32)
        carrier = sb("carrier", [P, 1], F32)
        expt = sb("expt", [P, 1], F32)
        root = sb("root", [P, 4], F32)
        ssw = sb("ssw", [P, 3], F32)
        amw = sb("amw", [P, 2], F32)
        nmean = sb("nmean", [P, TILES], F32)
        half = sb("half", [P, TILES], F32)
        nmax = sb("nmax", [P, UBUF, 4], F32)
        rsum = sb("rsum", [P, UBUF, 4], F32)
        rinv = sb("rinv", [P, UBUF, 4], F32)
        bnx = sb("bnx", [P, TILES, 6], F32)
        mvx = sb("mvx", [P, TILES, 2], F32)
        vex = sb("vex", [P, TILES], F32)
        rsx = sb("rsx", [P, TILES], F32)
        bny = sb("bny", [P, TILES, 6], F32)
        mvy = sb("mvy", [P, TILES, 2], F32)
        vey = sb("vey", [P, TILES], F32)
        rsy = sb("rsy", [P, TILES], F32)
        top8 = sb("top8", [P, TILES, 8], F32)
        rout = sb("rout", [P, TILES], F32)
        nbias = sb("nbias", [P, TILES], F32)
        SC, TK, VL, WO, EX, GA, UP, DN = range(8)
        KO, KE, KY = range(3)

        bank = [ctx.enter_context(nc.psum_tensor(f"bank{i}", [P, 512], F32)) for i in range(8)]
        psY, psU, psS, psT = bank[0:4], bank[4:6], bank[6], bank[7]

        def alone_bank(u):
            return psU[0] if u == UNITS - 1 else psU[1]

        count_bank = bank[0:3] + [psS]

        ld = {n: sem("ld_" + n) for n in ("idc", "emb", "nw", "proj", "wq", "wk", "wv", "bqk", "bv", "bo",
                                          "wo", "up0", "up1", "up2", "up3", "gate", "ex", "dn", "gam")}
        s_iota, s_pool0, s_dve, s_act = sem("s_iota"), sem("s_pool0"), sem("s_dve"), sem("s_act")
        s_ohr, s_cnt, s_lnraw, s_unseen, s_lnc = (sem(n) for n in ("s_ohr", "s_cnt", "s_lnraw", "s_unseen", "s_lnc"))
        s_var0, s_rs0, s_row, s_rowT, s_colT, s_proj, s_psb = (sem(n) for n in (
            "s_var0", "s_rs0", "s_row", "s_rowT", "s_colT", "s_proj", "s_psb"))
        s_qkv, s_qk, s_tab, s_ohT, s_oht = sem("s_qkv"), sem("s_qk"), sem("s_tab"), sem("s_ohT"), sem("s_oht")
        s_tsum, s_upsc, s_dnsc, s_dnraw, s_gram, s_exsc, s_vsum, s_ssq, s_ams, s_ssw, s_amw = (sem(n) for n in ("s_tsum", "s_upsc", "s_dnsc", "s_dnraw", "s_gram", "s_exsc", "s_vsum", "s_ssq", "s_ams", "s_ssw", "s_amw"))
        s_mx, s_am, s_scl = sem("s_mx"), sem("s_am"), sem("s_scl")
        s_hi, s_lo, s_val = sem("s_hi"), sem("s_lo"), sem("s_val")
        s_whi, s_wlo, s_uphi, s_uplo, s_dnhi, s_dnlo = (sem(n) for n in (
            "s_whi", "s_wlo", "s_uphi", "s_uplo", "s_dnhi", "s_dnlo"))
        s_scored, s_added, s_max, s_exp, s_rec, s_norm, s_trn, s_pt = (sem(n) for n in (
            "s_scored", "s_added", "s_max", "s_exp", "s_rec", "s_norm", "s_trn", "s_pt"))
        s_pv, s_yh, s_yl = sem("s_pv"), sem("s_yh"), sem("s_yl")
        s_tg, s_wo, s_tokr, s_h1, s_bn, s_agg, s_ve, s_rs, s_x, s_xt, s_xh, s_xl, s_h1b = (sem(n) for n in (
            "s_tg", "s_wo", "s_tokr", "s_h1", "s_bn", "s_agg", "s_ve", "s_rs", "s_x", "s_xt", "s_xh", "s_xl", "s_h1b"))
        s_gate, s_top, s_rout, s_up, s_relu, s_sq, s_sh, s_sl, s_dn, s_ex, s_moe = (sem(n) for n in (
            "s_gate", "s_top", "s_rout", "s_up", "s_relu", "s_sq", "s_sh", "s_sl", "s_dn", "s_ex", "s_moe"))
        s_dt, s_yev, s_bny, s_aggy, s_vey, s_rsy, s_nb, s_zn, s_zg, s_fin, s_last = (sem(n) for n in (
            "s_dt", "s_yev", "s_bny", "s_aggy", "s_vey", "s_rsy", "s_nb", "s_zn", "s_zg", "s_fin", "s_last"))
        s_out = [sem("s_out0"), sem("s_out1")]

        def need(eng, s, value):
            if isinstance(value, int) and value <= 0:
                return
            eng.wait_ge(s, value)

        def bc(ap, n, dt_shape):
            return ap.unsqueeze(1).broadcast_to(dt_shape)

        block = ctx.enter_context(nc.Block())

        @block.sync
        def _(sp):
            for b in range(2):
                sp.sem_inc(s_out[b], 16)

            def load(dst, src, name):
                sp.dma_start(dst, src).then_inc(ld[name], 16)

            load(row, emb, "emb")
            load(idc[:, :].bitcast(I32), ids_col, "idc")
            load(nrm, norm_w.partition_broadcast(P), "nw")
            load(pj_sb, proj_t.rearrange("(k p) n -> p k n", p=P), "proj")
            for k in range(2):
                load(rawu[:, k * INTER:(k + 1) * INTER], up[k * P:(k + 1) * P, :], f"up{k}")
            load(wq_sb, wq.rearrange("(k p) n -> p k n", p=P), "wq")
            load(bo_sb, bo.partition_broadcast(P), "bo")
            load(bqk[:, 0], bq, "bqk")
            load(bqk[:, 1], bk, "bqk")
            load(wk_sb, wk.rearrange("(k p) n -> p k n", p=P), "wk")
            for k in range(2, KC):
                load(rawu[:, k * INTER:(k + 1) * INTER], up[k * P:(k + 1) * P, :], f"up{k}")
            load(wv_sb, wv.rearrange("(k p) n -> p k n", p=P), "wv")
            load(bv_sb, bv.partition_broadcast(P), "bv")
            load(raww, wo.rearrange("(k p) n -> p k n", p=P), "wo")
            load(rawe, expert.rearrange("(k p) n -> p k n", p=P), "ex")
            load(rawg[:, :, :], gate.rearrange("(k p) n -> p k n", p=P), "gate")
            load(rawd[:, :].rearrange("p (k n) -> p k n", k=IC), down.rearrange("(k p) n -> p k n", p=P), "dn")
            sp.wait_ge(s_dnlo, 4)
            load(gam, gamma.partition_broadcast(P), "gam")
            load(bet, beta.partition_broadcast(P), "gam")

            def store(j, g, rows):
                sp.dma_start(out[bass.ds(g * GT + j * P, P), :], rows).then_inc(s_out[j % 2], 16)

            with sp.Fori(0, GROUPS - 1) as g:
                for j in range(TILES):
                    sp.wait_ge(s_fin, g * TILES + j + 1)
                    store(j, g, fin[:, j % 2])
            for j, done, count in ((0, s_fin, (GROUPS - 1) * TILES + 1), (2, s_last, 1),
                                   (1, s_fin, (GROUPS - 1) * TILES + 2), (3, s_last, 2)):
                sp.wait_ge(done, count)
                store(j, GROUPS - 1, h1[:, j])
            for b in range(2):
                sp.wait_ge(s_out[b], 16 * (GROUPS * TILES // 2 + 1))

        @block.gpsimd
        def _(pool):
            nc.gpsimd.iota(iota_vi, [[1, P]], base=0, channel_multiplier=0).then_inc(s_iota, 1)
            nc.gpsimd.memset(half[:, :], -0.5).then_inc(s_pool0, 1)
            nc.gpsimd.memset(root[:, :], 0.5).then_inc(s_pool0, 1)
            nc.gpsimd.memset(ident[:, :], 0.0).then_inc(s_pool0, 1)
            nc.gpsimd.memset(identh, 0.0).then_inc(s_pool0, 1)
            nc.gpsimd.memset(ones[:, :], 1.0).then_inc(s_pool0, 1)
            nc.gpsimd.memset(lnb[:, 0:1], TINY).then_inc(s_pool0, 1)
            nc.gpsimd.memset(lnb[:, 1:2], -10 * UNSEEN).then_inc(s_pool0, 1)
            pool.wait_ge(s_pool0, 7)
            for m in (ident[:, :], identh):
                nc.gpsimd.affine_select(out=m, in_=m, compare_op=ALU.not_equal, fill=1.0, base=0,
                                        pattern=[[-1, P]], channel_multiplier=1).then_inc(s_pool0, 1)
            nc.gpsimd.affine_select(out=tri[:, :], in_=ones[:, :], compare_op=ALU.is_ge, fill=0.0, base=0,
                                    pattern=[[1, P]], channel_multiplier=-1).then_inc(s_pool0, 1)

            def rsqrt(dst, src, n):
                return nc.gpsimd.tensor_tensor(dst, src, half[:, 0:n], ALU.pow)

            def all_largest(dst, src, n):
                pool.wait_ge(s_mx, n)
                nc.gpsimd.partition_all_reduce(dst, src, P, ABSMAX).then_inc(s_am, 1)

            def token_norm(i):
                pool.wait_ge(s_var0, i + 1)
                rsqrt(stat[:, 1, i:i + 1], stat[:, 0, i:i + 1], 1).then_inc(s_rs0, 1)

            token_norm(0)
            pool.wait_ge(s_ohr, 1)
            tiles = [ohr[:, 4 * b:4 * b + 4, :].rearrange("p j v -> p (j v)") for b in range(3)]
            nc.gpsimd.tensor_tensor(ohr_sum[:, 0], tiles[0], tiles[1], ALU.add).then_inc(s_tsum, 1)
            pool.wait_ge(s_tsum, 1)
            nc.gpsimd.tensor_tensor(ohr_sum[:, 1], ohr_sum[:, 0], tiles[2], ALU.add).then_inc(s_tsum, 1)
            token_norm(1)
            token_norm(2)
            all_largest(am[:, UP:UP + 1], mx[:, UP:UP + 1], 1)
            all_largest(am[:, SC:TK + 1], mx[:, SC:TK + 1], 2)

            def up_low(k):
                raw = rawu[:, k * INTER:(k + 1) * INTER]
                pool.wait_ge(s_uphi, k + 1)
                if k >= UP_SCALED:
                    nc.gpsimd.tensor_tensor(raw, raw, scl[:, UP:UP + 1].broadcast_to([P, INTER]), ALU.mult).then_inc(s_upsc, 1)
                    pool.wait_ge(s_upsc, k - UP_SCALED + 1)
                nc.gpsimd.tensor_tensor(up_hl[:, 1, k], raw, up_hl[:, 0, k], ALU.subtract).then_inc(s_uplo, 1)

            up_low(0)
            up_low(1)
            pool.wait_ge(s_mx, 3)
            nc.gpsimd.partition_all_reduce(am[:, VL:VL + 1], mx[:, VL:VL + 1], P, ABSMAX).then_inc(s_amw, 1)
            nc.gpsimd.partition_all_reduce(am[:, GA:GA + 1], mx[:, GA:GA + 1], P, ABSMAX).then_inc(s_amw, 1)
            pool.wait_ge(s_ssw, 2)
            nc.gpsimd.partition_all_reduce(amw[:, :], ssw[:, 0:2], P, ABSMAX).then_inc(s_amw, 1)
            pool.wait_ge(s_amw, 3)
            nc.gpsimd.tensor_tensor(am[:, WO:EX + 1], amw[:, :], root[:, 0:2], ALU.pow).then_inc(s_am, 1)
            up_low(2)
            pool.wait_ge(s_ssw, 3)
            nc.gpsimd.partition_all_reduce(ams[:, :], ssw[:, 2:3], P, ABSMAX).then_inc(s_ams, 1)
            pool.wait_ge(s_ams, 1)
            nc.gpsimd.tensor_tensor(am[:, DN:DN + 1], ams[:, :], root[:, 0:1], ALU.pow).then_inc(s_am, 1)
            up_low(3)

            def down_scaled(k):
                raw = rawd[:, k * 2048:(k + 1) * 2048]
                pool.wait_ge(s_dnhi, k + 1)
                nc.gpsimd.tensor_tensor(raw, raw, scl[:, DN:DN + 1].broadcast_to([P, INTER]), ALU.mult).then_inc(s_dnsc, 1)

            def down_low(k):
                if k < IC // 4 - 1:
                    pool.wait_ge(s_dnsc, k + 1)
                else:
                    pool.wait_ge(s_dnraw, 1)
                nc.gpsimd.tensor_tensor(dn_hl[:, 1, 4 * k:4 * k + 4],
                                        rawd[:, k * 2048:(k + 1) * 2048].rearrange("p (k n) -> p k n", k=4),
                                        dn_hl[:, 0, 4 * k:4 * k + 4], ALU.subtract).then_inc(s_dnlo, 1)

            def row_norm(j, g):
                pool.wait_ge(s_ve, g * TILES + j + 1)
                rsqrt(rsx[:, j:j + 1], vex[:, j:j + 1], 1).then_inc(s_rs, 1)

            down_scaled(0)
            row_norm(0, 0)
            down_low(0)
            down_scaled(1)
            down_low(1)
            row_norm(1, 0)
            down_scaled(2)
            down_low(2)
            down_low(3)
            row_norm(2, 0)
            row_norm(3, 0)
            pool.wait_ge(s_whi, 3)
            raw, high, low = (w.rearrange("p k n -> p (k n)") for w in (rawe, ex_hl[:, 0], ex_hl[:, 1]))
            nc.gpsimd.tensor_tensor(raw, raw, scl[:, EX:EX + 1].broadcast_to([P, KC * DM]), ALU.mult).then_inc(s_exsc, 1)
            pool.wait_ge(s_exsc, 1)
            nc.gpsimd.tensor_tensor(low, raw, high, ALU.subtract).then_inc(s_exsc, 1)

            def shared_norm(pair, g):
                c = slice(2 * pair, 2 * pair + 2)
                pool.wait_ge(s_vey, 2 * g + pair + 1)
                rsqrt(rsy[:, c], vey[:, c], 2).then_inc(s_rsy, 1)
                pool.wait_ge(s_rsy, 2 * g + pair + 1)
                nc.gpsimd.tensor_tensor(nbias[:, c], nmean[:, c], rsy[:, c], ALU.mult).then_inc(s_nb, 1)

            def row_plus_beta(j, g):
                nc.gpsimd.tensor_tensor(h1b[:, j], h1[:, j], bet, ALU.add).then_inc(s_h1b, 1)

            def finish(j, g):
                pool.wait_ge(s_zn, g * TILES + j + 1)
                nc.gpsimd.tensor_tensor(y[:, j], y[:, j], gam, ALU.mult).then_inc(s_zg, 1)
                pool.wait_ge(s_zg, g * TILES + j + 1)
                pool.wait_ge(s_out[j % 2], g * (8 * TILES) + (j // 2 + 1) * 16)
                nc.gpsimd.tensor_tensor(fin[:, j % 2], y[:, j], h1b[:, j], ALU.add).then_inc(s_fin, 1)

            pool.wait_ge(ld["gam"], 32)
            pool.wait_ge(s_h1, TILES)
            for j in range(TILES):
                row_plus_beta(j, 0)
            with pool.Fori(0, GROUPS - 1) as g:
                for j in range(TILES - 1):
                    row_norm(j, g + 1)
                shared_norm(0, g)
                row_norm(TILES - 1, g + 1)
                shared_norm(1, g)
                for j in range(TILES):
                    finish(j, g)
                    pool.wait_ge(s_fin, g * TILES + j + 1)
                    row_plus_beta(j, g + 1)
            before = 2 * (GROUPS - 1)
            tiles = (GROUPS - 1) * TILES

            def last_rsqrt(j):
                pool.wait_ge(s_vey, before + j + 1)
                rsqrt(rsy[:, j:j + 1], vey[:, j:j + 1], 1).then_inc(s_rsy, 1)

            def last_bias(j):
                last_rsqrt(j)
                pool.wait_ge(s_rsy, before + j + 1)
                nc.gpsimd.tensor_tensor(nbias[:, j:j + 1], nmean[:, j:j + 1], rsy[:, j:j + 1], ALU.mult).then_inc(s_nb, 1)

            def last_scaled(j):
                pool.wait_ge(s_zn, tiles + j + 1)
                nc.gpsimd.tensor_tensor(y[:, j], y[:, j], gam, ALU.mult).then_inc(s_zg, 1)

            def last_sum(j):
                pool.wait_ge(s_zg, tiles + j + 1)
                nc.gpsimd.tensor_tensor(h1[:, j], y[:, j], h1b[:, j], ALU.add).then_inc(s_fin, 1)

            last_bias(0)
            last_scaled(0)
            last_bias(1)
            last_sum(0)
            last_rsqrt(2)
            last_scaled(1)
            last_rsqrt(3)
            last_sum(1)

        @block.scalar
        def _(act):
            def copy(dst, src, scale=None):
                if scale is None:
                    return nc.scalar.copy(dst, src)
                return nc.scalar.activation(dst, src, ACT.Copy, scale=scale)

            act.wait_ge(s_rowT, 1)
            copy(colT, psS[:, :]).then_inc(s_colT, 1)
            act.wait_ge(s_proj, 1)
            copy(tok[:, :], psT[:, :]).then_inc(s_psb, 1)

            def ln_counts(b):
                act.wait_ge(s_cnt, b + 1)
                nc.scalar.activation(lnc[:, 4 * b:4 * b + 4, :].rearrange("p j v -> p (j v)"), count_bank[b][:, :], ACT.Ln,
                                     bias=lnb[:, 0:1]).then_inc(s_lnraw, 1)

            def push_down(b):
                act.wait_ge(s_lnraw, b + 1)
                nc.scalar.activation(unseen[:, b], lnc[:, 4 * b:4 * b + 4, :].rearrange("p j v -> p (j v)"), ACT.Relu,
                                     bias=lnb[:, 1:2], scale=-UNSEEN).then_inc(s_unseen, 1)

            ln_counts(0)
            ln_counts(1)
            for b in range(2):
                act.wait_ge(s_ohT, b + 1)
                copy(oht[:, b * 1024:(b + 1) * 1024], psU[b][:, :].bitcast(F16)).then_inc(s_oht, 1)
            push_down(0)
            act.wait_ge(s_rowT, 2)
            copy(colT, psS[:, :]).then_inc(s_colT, 1)
            ln_counts(2)
            push_down(1)
            push_down(2)
            ln_counts(3)
            push_down(3)
            nc.scalar.activation(expt[:, :], half[:, 0:1], ACT.Exp)

            def up_high(k):
                act.wait_ge(s_scl, 1)
                last = copy(up_hl[:, 0, k], rawu[:, k * INTER:(k + 1) * INTER], scl[:, UP:UP + 1])
                if k >= UP_SCALED:
                    last.then_inc(s_uphi, 1)

            def up_scaled(k):
                raw = rawu[:, k * INTER:(k + 1) * INTER]
                copy(raw, raw, scl[:, UP:UP + 1]).then_inc(s_uphi, 1)

            up_high(0)
            up_scaled(0)
            act.wait_ge(s_scl, 2)
            for j in range(4):
                copy(sc_hl[:, 0].rearrange("p (c j) v -> p c j v", j=4)[:, :, j, :],
                     bank[j][:, :].rearrange("p (c v) -> p c v", v=P), scl[:, SC:SC + 1]).then_inc(s_hi, 1)
            up_high(1)

            def output_high():
                act.wait_ge(s_scl, 3)
                copy(wo_hl[:, 0], raww, scl[:, WO:WO + 1]).then_inc(s_whi, 1)

            def expert_high():
                act.wait_ge(s_vsum, 1)
                copy(ex_hl[:, 0], rawe, scl[:, EX:EX + 1]).then_inc(s_whi, 1)

            def down_high(k):
                act.wait_ge(s_scl, 4)
                copy(dn_hl[:, 0, 4 * k:4 * k + 4].rearrange("p k n -> p (k n)"), rawd[:, k * 2048:(k + 1) * 2048],
                     scl[:, DN:DN + 1]).then_inc(s_dnhi, 1)

            def exps(u, g):
                act.wait_ge(s_max, g * UNITS + u + 1)
                for h in range(4):
                    last = nc.scalar.activation(prob[:, u % UBUF, h, :], prob[:, u % UBUF, h, :], ACT.Exp,
                                                bias=nmax[:, u % UBUF, h:h + 1], accum_out=rsum[:, u % UBUF, h:h + 1])
                last.then_inc(s_exp, 1)

            def evac_probs_alone(u):
                act.wait_ge(s_trn, u + 1)
                copy(probT0[:, u % UBUF], alone_bank(u)[:, :].rearrange("p (h t) -> p h t", h=4)).then_inc(s_pt, 1)

            def evac_y_alone(j):
                act.wait_ge(s_pv, j + 1)
                act.wait_ge(s_wlo, 1)
                copy(yt_hl[:, 0, :, j * P:(j + 1) * P], (psT, psY[3])[j % 2][:, :].rearrange("p (q t) -> p q t", q=HQ)).then_inc(s_yh, 1)

            def evac_probs(u, g):
                q, j = u // TILES, u % TILES
                ps = psT
                act.wait_ge(s_trn, g * UNITS + u + 1)
                if u == TILES:
                    act.wait_ge(s_exsc, 2)
                if q >= 2 and j == 0:
                    act.wait_ge(s_pv, g * HQ + q - 1)
                copy(probT[:, q % 2, :, j * P:(j + 1) * P],
                     ps[:, :].rearrange("p (h t) -> p h t", h=4)).then_inc(s_pt, 1)

            def evac_y(q, g):
                act.wait_ge(s_pv, g * HQ + q + 1)
                copy(yt_hl[:, 0, q], psT[:, :]).then_inc(s_yh, 1)

            def token_rows(j, g, ps=psS):
                act.wait_ge(s_tg, g * TILES + j + 1)
                if j >= 2:
                    act.wait_ge(s_h1, g * TILES + j - 1)
                copy(tokr[:, j % 2], ps[:, :], inv[:, TK:TK + 1]).then_inc(s_tokr, 1)

            def split_x(j, g, ps):
                act.wait_ge(s_xt, g * TILES + j + 1)
                copy(xt_hl[:, 0, :, j * P:(j + 1) * P],
                     ps[:, :].rearrange("p (k t) -> p k t", k=KC)).then_inc(s_xh, 1)

            def square(i, g):
                act.wait_ge(s_up, g * IC + i + 1)
                nc.scalar.activation(relu[:, i % 2], psU[i % 2][:, :], ACT.Relu,
                                     scale=2.0 ** -(XSHIFT + RSHIFT)).then_inc(s_relu, 1)
                act.wait_ge(s_relu, g * IC + i + 1)
                if i >= 2:
                    act.wait_ge(s_sl, g * IC + i - 1)
                nc.scalar.activation(sqr[:, i % 2], relu[:, i % 2], ACT.Square).then_inc(s_sq, 1)
                act.wait_ge(s_sq, g * IC + i + 1)
                if i >= RING:
                    act.wait_ge(s_dn, g * (IC - 1) + i - RING + 1)
                copy(sq_hl[:, i % RING, 0], sqr[:, i % 2]).then_inc(s_sh, 1)

            def norm_rows(j):
                nc.scalar.activation(y[:, j], y[:, j], ACT.Identity, scale=rsy[:, j:j + 1],
                                     bias=nbias[:, j:j + 1]).then_inc(s_zn, 1)

            def shared_norm(j, g):
                act.wait_ge(s_nb, 2 * g + j // 2 + 1)
                norm_rows(j)

            exps(0, 0)
            exps(1, 0)
            for u in range(UNITS):
                if u < UNITS - 2:
                    exps(u + 2, 0)
                evac_probs_alone(u)
                j, step = u // HQ - 1, u % HQ
                if step == 0 and j >= 0:
                    evac_y_alone(j)
                if step == 1 and j >= 1:
                    act.wait_ge(s_uplo, KC)
                    split_x(j - 1, 0, psU[0])
                if step == 2 and j >= 0:
                    act.wait_ge(s_uplo, 1)
                    token_rows(j, 0)
                if u in (0, 3):
                    up_high(2 + u // 3)
                if u == 1:
                    copy(tk_hl[:, 0], tok[:, :], scl[:, TK:TK + 1]).then_inc(s_hi, 1)
                if u == 2:
                    output_high()
                if u in DN_UNITS:
                    down_high(DN_UNITS.index(u))
                if u == RAW_UNIT:
                    raw = rawd[:, 3 * 2048:4 * 2048]
                    copy(raw, raw, scl[:, DN:DN + 1]).then_inc(s_dnraw, 1)
                if u == EXPERT_UNIT:
                    expert_high()
            evac_y_alone(TILES - 1)
            token_rows(TILES - 1, 0)
            split_x(TILES - 2, 0, psU[0])
            split_x(TILES - 1, 0, psU[0])
            act.wait_ge(s_dnlo, 4)
            square(0, 0)
            with act.Fori(0, GROUPS - 1) as g:
                for i in range(IC):
                    if i > 0:
                        square(i, g)
                    if i > TILES and i % TILES == 1:
                        evac_y(i // TILES - 1, g + 1)
                    exps(i, g + 1)
                    if i > 0:
                        evac_probs(i - 1, g + 1)
                evac_probs(UNITS - 1, g + 1)
                evac_y(HQ - 1, g + 1)
                for j in range(3):
                    token_rows(j, g + 1)
                split_x(0, g + 1, psY[0])
                token_rows(3, g + 1)
                split_x(1, g + 1, psY[1])
                split_x(2, g + 1, psY[0])
                shared_norm(0, g)
                shared_norm(1, g)
                split_x(3, g + 1, psY[1])
                square(0, g + 1)
                shared_norm(2, g)
                shared_norm(3, g)
            for i in range(1, IC):
                square(i, GROUPS - 1)
            for j in range(2):
                act.wait_ge(s_nb, 2 * (GROUPS - 1) + j + 1)
                norm_rows(j)

        @block.vector
        def _(dve):
            chain = [0]

            def link(ins):
                chain[0] += 1
                ins.then_inc(s_dve, 1)
                dve.wait_ge(s_dve, chain[0])

            def largest(col, src, ax):
                return nc.vector.tensor_reduce(mx[:, col:col + 1], src, ax, ALU.max, apply_absolute_value=True)

            def wrap(ids_i, f, t):
                link(nc.vector.tensor_scalar(t, ids_i, 0.0, float(P), ALU.is_lt, ALU.mult))
                link(nc.vector.tensor_tensor(f, ids_i, t, ALU.add))
                link(nc.vector.tensor_scalar(f, f, float(P - 1), 0.0, ALU.min, ALU.max))

            def scales(a, b, n):
                dve.wait_ge(s_am, n)
                link(nc.vector.tensor_scalar(p2[:, a:b], am[:, a:b], 2.0 ** -100, 2.0 ** 100, ALU.max, ALU.min))
                link(nc.vector.tensor_scalar(p2[:, a:b].bitcast(I32), p2[:, a:b].bitcast(I32), 0x7F800000, None,
                                             ALU.bitwise_and))
                link(nc.vector.tensor_scalar(inv[:, a:b], p2[:, a:b], 2.0 ** -TOP, None, ALU.mult))
                link(nc.vector.tensor_scalar(scl[:, a:b].bitcast(I32), p2[:, a:b].bitcast(I32), 0x7F800000, None,
                                             ALU.bitwise_xor))
                link(nc.vector.tensor_scalar(scl[:, a:b], scl[:, a:b], 2.0 ** (TOP - 1), None, ALU.mult))
                nc.vector.tensor_scalar(p2[:, a:b], scl[:, a:b], 1.0, None, ALU.mult).then_inc(s_scl, 1)

            def low(dst, src, high, col, s_high, s_low, n):
                dve.wait_ge(s_high, n)
                nc.vector.scalar_tensor_tensor(dst, src, scl[:, col:col + 1], high, ALU.mult,
                                               ALU.subtract).then_inc(s_low, 1)

            dve.wait_ge(s_iota, 1)
            link(nc.vector.tensor_copy(iota_v, iota_vi))
            dve.wait_ge(ld["idc"], 16)
            wrap(idc[:, :].bitcast(I32), tmpc2[:, :], tmpc[:, :])
            dve.wait_ge(ld["emb"], 16)
            link(nc.vector.tensor_tensor_reduce(out=tok[:, :], in0=row, in1=row, scale=1.0, scalar=0.0, op0=ALU.mult,
                                                op1=ALU.add, accum_out=stat[:, 0, 3:4]))
            nc.vector.tensor_scalar(stat[:, 0, 0:1], stat[:, 0, 3:4], 1.0 / DM, EPS_RMS, ALU.mult,
                                    ALU.add).then_inc(s_var0, 1)
            dve.wait_ge(ld["nw"], 16)
            dve.wait_ge(s_rs0, 1)
            nc.vector.scalar_tensor_tensor(row, row, stat[:, 1, 0:1], nrm, ALU.mult, ALU.mult).then_inc(s_row, 1)
            nc.vector.tensor_tensor(ohr, iota_v.unsqueeze(1).broadcast_to([P, SEQ // P, P]),
                                    tmpc2[:, :].unsqueeze(2).broadcast_to([P, SEQ // P, P]), ALU.is_equal).then_inc(s_ohr, 1)
            def up_largest(k):
                dve.wait_ge(ld[f"up{k}"], 16)
                link(nc.vector.tensor_reduce(mxs[:, k:k + 1], rawu[:, k * INTER:(k + 1) * INTER], AX.X, ALU.max,
                                             apply_absolute_value=True))

            up_largest(0)
            dve.wait_ge(s_psb, 1)
            link(nc.vector.tensor_tensor_reduce(out=nrm, in0=tok[:, :], in1=tok[:, :], scale=1.0, scalar=0.0,
                                                op0=ALU.mult, op1=ALU.add, accum_out=stat[:, 0, 3:4]))
            nc.vector.tensor_scalar(stat[:, 0, 1:2], stat[:, 0, 3:4], 1.0 / DM, EPS_RMS, ALU.mult,
                                    ALU.add).then_inc(s_var0, 1)
            dve.wait_ge(s_rs0, 2)
            link(nc.vector.tensor_scalar(tok[:, :], tok[:, :], stat[:, 1, 1:2], None, ALU.mult))
            link(nc.vector.bn_stats(bn0[:, :], tok[:, :]))
            link(nc.vector.bn_aggr(stat[:, 0, 4:6], bn0[:, :]))
            nc.vector.tensor_scalar(stat[:, 0, 2:3], stat[:, 0, 5:6], EPS_LN, None, ALU.add).then_inc(s_var0, 1)
            dve.wait_ge(s_rs0, 3)
            nc.vector.tensor_scalar(row, tok[:, :], stat[:, 0, 4:5], stat[:, 1, 2:3], ALU.subtract,
                                    ALU.mult).then_inc(s_row, 1)
            dve.wait_ge(ld["bo"], 16)
            dve.wait_ge(s_row, 2)
            link(nc.vector.tensor_tensor(tok[:, :], tok[:, :], bo_sb, ALU.add))
            link(largest(TK, tok[:, :], AX.X))
            up_largest(1)

            def counts_done(b):
                lb = lnc[:, 4 * b:4 * b + 4, :].rearrange("p j v -> p (j v)")
                dve.wait_ge(s_unseen, b + 1)
                nc.vector.tensor_tensor(lb, lb, unseen[:, b], ALU.subtract).then_inc(s_lnc, 1)

            counts_done(0)
            dve.wait_ge(ld["bqk"], 32)
            dve.wait_ge(s_qkv, 1)
            for m in range(KC):
                last = nc.vector.tensor_scalar(qT[:, m], psU[0][:, m * P:(m + 1) * P], bqk[:, 0, m:m + 1], float(HD) ** -0.5,
                                               ALU.add, ALU.mult)
            last.then_inc(s_qk, 1)
            up_largest(2)
            dve.wait_ge(s_qkv, 2)
            for m in range(KC):
                last = nc.vector.tensor_scalar(kT[:, m], psU[1][:, m * P:(m + 1) * P], bqk[:, 1, m:m + 1], None, ALU.add)
            last.then_inc(s_qk, 1)
            up_largest(3)
            largest(UP, mxs[:, :], AX.X).then_inc(s_mx, 1)
            dve.wait_ge(s_mx, 1)
            scales(UP, UP + 1, 1)
            dve.wait_ge(s_tab, 1)
            for j in range(4):
                link(nc.vector.tensor_reduce(mxs[:, j:j + 1], bank[j][:, :], AX.X, ALU.max, apply_absolute_value=True))
            largest(SC, mxs[:, :], AX.X).then_inc(s_mx, 1)
            scales(SC, TK + 1, 2)
            dve.wait_ge(s_qkv, 3)
            dve.wait_ge(ld["bv"], 16)
            nc.vector.tensor_tensor(val[:, :], psT[:, :], bv_sb, ALU.add).then_inc(s_vsum, 1)
            dve.wait_ge(ld["gate"], 16)
            link(largest(GA, rawg[:, :, :], AX.XY))
            for j in range(4):
                low(sc_hl[:, 1].rearrange("p (c j) v -> p c j v", j=4)[:, :, j, :],
                    bank[j][:, :].rearrange("p (c v) -> p c v", v=P),
                    sc_hl[:, 0].rearrange("p (c j) v -> p c j v", j=4)[:, :, j, :], SC, s_hi, s_lo, j + 1)
            dve.wait_ge(s_vsum, 1)
            largest(VL, val[:, :], AX.X).then_inc(s_mx, 1)

            def output_low():
                low(wo_hl[:, 1], raww, wo_hl[:, 0], WO, s_whi, s_wlo, 1)

            def gate_split():
                nc.vector.tensor_scalar(gt_hl[:, 0], rawg[:, :, :], scl[:, GA:GA + 1], None, ALU.mult).then_inc(s_whi, 1)
                low(gt_hl[:, 1], rawg[:, :, :], gt_hl[:, 0], GA, s_whi, s_wlo, 3)

            def undo_factors(which):
                if which == KO:
                    link(nc.vector.tensor_scalar(kap[:, KO:KO + 1], inv[:, VL:VL + 1], inv[:, WO:WO + 1], None, ALU.mult))
                    return
                link(nc.vector.tensor_scalar(kap[:, KE:KE + 1], inv[:, GA:GA + 1], inv[:, EX:EX + 1],
                                             2.0 ** (-2 * XSHIFT), ALU.mult, ALU.mult))
                link(nc.vector.tensor_scalar(kap[:, KY:KY + 1], inv[:, UP:UP + 1], 2.0 ** RSHIFT, None, ALU.mult))
                link(nc.vector.tensor_scalar(kap[:, KY:KY + 1], kap[:, KY:KY + 1], kap[:, KY:KY + 1], inv[:, DN:DN + 1],
                                             ALU.mult, ALU.mult))

            def column_squares(n, ps):
                dve.wait_ge(s_gram, n + 1)
                need(dve, s_ssw, n - 1)
                nc.vector.tensor_tensor_reduce(out=scrap[:, n % 2], in0=ps[:, :].rearrange("p (c v) -> p c v", c=KC),
                                               in1=ident[:, :].unsqueeze(1).broadcast_to([P, KC, P]), scale=1.0,
                                               scalar=0.0, op0=ALU.mult, op1=ALU.add,
                                               accum_out=ssw[:, n:n + 1]).then_inc(s_ssw, 1)

            def carry_wait():
                nc.vector.tensor_copy(carrier[:, :], half[:, 0:1])

            def bias_and_max(u, g, ps=psS, tile=None):
                if tile is None:
                    tile = g * TILES + u % TILES
                dve.wait_ge(s_scored, g * UNITS + u + 1)
                need(dve, s_trn, g * UNITS + u + 1 - UBUF)
                nc.vector.scalar_tensor_tensor(
                    prob[:, u % UBUF], ps[:, :].rearrange("p (h v) -> p h v", h=4), inv[:, SC:SC + 1],
                    lnc[:, bass.ds(tile, 1), :].broadcast_to([P, 4, P]), ALU.mult, ALU.add).then_inc(s_added, 1)
                dve.wait_ge(s_added, g * UNITS + u + 1)
                nc.vector.tensor_reduce(nmax[:, u % UBUF], prob[:, u % UBUF], AX.X, ALU.max, negate=True).then_inc(s_max, 1)

            def normalise(u, g):
                dve.wait_ge(s_exp, g * UNITS + u + 1)
                nc.vector.reciprocal(rinv[:, u % UBUF], rsum[:, u % UBUF]).then_inc(s_rec, 1)
                dve.wait_ge(s_rec, g * UNITS + u + 1)
                nc.vector.tensor_tensor(prob[:, u % UBUF], prob[:, u % UBUF],
                                        rinv[:, u % UBUF].unsqueeze(2).broadcast_to([P, 4, P]), ALU.mult).then_inc(s_norm, 1)

            def low_y(q, g):
                dve.wait_ge(s_yh, g * HQ + q + 1)
                nc.vector.tensor_tensor(yt_hl[:, 1, q], psT[:, :], yt_hl[:, 0, q], ALU.subtract).then_inc(s_yl, 1)

            def low_y_alone(j):
                dve.wait_ge(s_yh, j + 1)
                t = slice(j * P, (j + 1) * P)
                nc.vector.tensor_tensor(yt_hl[:, 1, :, t], (psT, psY[3])[j % 2][:, :].rearrange("p (q t) -> p q t", q=HQ),
                                        yt_hl[:, 0, :, t], ALU.subtract).then_inc(s_yl, 1)

            def residual(j, g, ps):
                dve.wait_ge(s_wo, g * TILES + j + 1)
                dve.wait_ge(s_tokr, g * TILES + j + 1)
                need(dve, s_h1b, g * TILES)
                nc.vector.scalar_tensor_tensor(h1[:, j], ps[:, :], kap[:, KO:KO + 1], tokr[:, j % 2], ALU.mult,
                                               ALU.add).then_inc(s_h1, 1)
                dve.wait_ge(s_h1, g * TILES + j + 1)
                nc.vector.bn_stats(bnx[:, j], h1[:, j]).then_inc(s_bn, 1)
                dve.wait_ge(s_bn, g * TILES + j + 1)
                carry_wait()
                nc.vector.bn_aggr(mvx[:, j], bnx[:, j]).then_inc(s_agg, 1)
                dve.wait_ge(s_agg, g * TILES + j + 1)
                nc.vector.tensor_scalar(vex[:, j:j + 1], mvx[:, j, 1:2], EPS_LN, 2.0 ** (-2 * XSHIFT), ALU.add,
                                        ALU.mult).then_inc(s_ve, 1)

            def layer_norm(j, g):
                dve.wait_ge(s_rs, g * TILES + j + 1)
                if j >= 2:
                    dve.wait_ge(s_xt, g * TILES + j - 1)
                nc.vector.tensor_scalar(xrow[:, j % 2], h1[:, j], mvx[:, j, 0:1], rsx[:, j:j + 1], ALU.subtract,
                                        ALU.mult).then_inc(s_x, 1)

            def low_x(j, g, ps):
                dve.wait_ge(s_xh, g * TILES + j + 1)
                c = slice(j * P, (j + 1) * P)
                nc.vector.tensor_tensor(xt_hl[:, 1, :, c], ps[:, :].rearrange("p (k t) -> p k t", k=KC),
                                        xt_hl[:, 0, :, c], ALU.subtract).then_inc(s_xl, 1)

            def largest_logits(g):
                dve.wait_ge(s_gate, g + 1)
                carry_wait()
                for j in range(TILES):
                    last = nc.vector.max(top8[:, j], psS[:, j * NEXP:(j + 1) * NEXP])
                last.then_inc(s_top, 1)

            def routing(g):
                dve.wait_ge(s_top, g + 1)
                for j in range(TILES):
                    last = nc.vector.tensor_scalar(rout[:, j:j + 1], top8[:, j, 0:1], top8[:, j, 1:2], kap[:, KE:KE + 1],
                                                   ALU.add, ALU.mult)
                last.then_inc(s_rout, 1)

            def low_square(i, g):
                dve.wait_ge(s_sh, g * IC + i + 1)
                nc.vector.tensor_tensor(sq_hl[:, i % RING, 1], sqr[:, i % 2], sq_hl[:, i % RING, 0],
                                        ALU.subtract).then_inc(s_sl, 1)

            def expert_rows(j, g, ps=None):
                if j == 0:
                    dve.wait_ge(s_rout, g + 1)
                dve.wait_ge(s_h1b, g * TILES + j + 1)
                dve.wait_ge(s_ex, g * TILES + j + 1)
                nc.vector.tensor_scalar(y[:, j], (ps or psU[EXPERT_BANK[j]])[:, :], rout[:, j:j + 1], None, ALU.mult).then_inc(s_moe, 1)

            def shared_sum(j, g):
                dve.wait_ge(s_dt, g * TILES + j + 1)
                dve.wait_ge(s_moe, g * TILES + j + 1)
                nc.vector.scalar_tensor_tensor(y[:, j], psY[j][:, :], kap[:, KY:KY + 1], y[:, j], ALU.mult,
                                               ALU.add).then_inc(s_yev, 1)

            def shared_stats(j, g):
                dve.wait_ge(s_yev, g * TILES + j + 1)
                nc.vector.bn_stats(bny[:, j], y[:, j]).then_inc(s_bny, 1)

            def shared_rows(j, g):
                shared_sum(j, g)
                shared_stats(j, g)

            def shared_norm(pair, g):
                c = slice(2 * pair, 2 * pair + 2)
                dve.wait_ge(s_bny, g * TILES + 2 * pair + 2)
                carry_wait()
                for j in (2 * pair, 2 * pair + 1):
                    last = nc.vector.bn_aggr(mvy[:, j], bny[:, j])
                last.then_inc(s_aggy, 1)
                dve.wait_ge(s_aggy, 2 * g + pair + 1)
                nc.vector.tensor_scalar(nmean[:, c], mvy[:, c, 0], -1.0, None, ALU.mult)
                nc.vector.tensor_scalar(vey[:, c], mvy[:, c, 1], EPS_LN, None, ALU.add).then_inc(s_vey, 1)

            def last_rows(j, g):
                shared_rows(j, g)
                dve.wait_ge(s_bny, g * TILES + j + 1)
                link(nc.vector.bn_aggr(mvy[:, j], bny[:, j]))
                if j < 2:
                    nc.vector.tensor_scalar(nmean[:, j:j + 1], mvy[:, j, 0:1], -1.0, None, ALU.mult)
                nc.vector.tensor_scalar(vey[:, j:j + 1], mvy[:, j, 1:2], EPS_LN, None, ALU.add).then_inc(s_vey, 1)

            def last_scaled(j):
                link(nc.vector.scalar_tensor_tensor(y[:, j], y[:, j], mvy[:, j, 0:1], gam, ALU.subtract, ALU.mult))

            def last_sum(j, g):
                dve.wait_ge(s_rsy, 2 * g + j + 1)
                dve.wait_ge(s_h1b, g * TILES + j + 1)
                nc.vector.scalar_tensor_tensor(h1[:, j], y[:, j], rsy[:, j:j + 1], h1b[:, j], ALU.mult,
                                               ALU.add).then_inc(s_last, 1)

            for u in range(3):
                bias_and_max(u, 0, psY[u % 2], u // HQ)
            for u in range(UNITS):
                normalise(u, 0)
                if u < UNITS - 3:
                    bias_and_max(u + 3, 0, psY[(u + 3) % 2], (u + 3) // HQ)
                j, step = u // HQ - 1, u % HQ
                if step == 0 and j >= 1:
                    layer_norm(j - 1, 0)
                if step == 1 and j >= 0:
                    low_y_alone(j)
                if step == 2 and j >= 1:
                    low_x(j - 1, 0, psU[0])
                if u in (0, 1, 2):
                    counts_done(u + 1)
                if u == 0:
                    column_squares(0, psU[0])
                    column_squares(1, psS)
                if u == 2:
                    scales(VL, GA + 1, 3)
                    nc.vector.tensor_scalar(val[:, :], val[:, :], scl[:, VL:VL + 1], None, ALU.mult).then_inc(s_val, 1)
                    undo_factors(KO)
                if u == 3:
                    low(tk_hl[:, 1], tok[:, :], tk_hl[:, 0], TK, s_hi, s_lo, 5)
                    output_low()
                if u == 4:
                    column_squares(2, psU[0])
                if u == 5:
                    scales(DN, DN + 1, 4)
                if u == UNITS - 1:
                    gate_split()
                if step == 3 and 0 <= j < TILES - 2:
                    dve.wait_ge(s_uplo, 2)
                    residual(j, 0, psY[2])
            low_y_alone(TILES - 1)
            residual(TILES - 2, 0, psY[2])
            undo_factors(KE)
            layer_norm(TILES - 2, 0)
            residual(TILES - 1, 0, psY[0])
            low_x(TILES - 2, 0, psU[0])
            layer_norm(TILES - 1, 0)
            low_x(TILES - 1, 0, psU[0])
            largest_logits(0)
            routing(0)
            with dve.Fori(0, GROUPS - 1) as g:
                for i in range(IC):
                    if i > 0:
                        normalise(i - 1, g + 1)
                    bias_and_max(i, g + 1)
                    if i > TILES and i % TILES == 1:
                        low_y(i // TILES - 1, g + 1)
                    low_square(i, g)
                normalise(UNITS - 1, g + 1)
                expert_rows(0, g)
                expert_rows(1, g)
                low_y(HQ - 1, g + 1)
                expert_rows(2, g)
                residual(0, g + 1, psT)
                shared_rows(0, g)
                residual(1, g + 1, psU[1])
                layer_norm(0, g + 1)
                shared_rows(1, g)
                residual(2, g + 1, psT)
                layer_norm(1, g + 1)
                low_x(0, g + 1, psY[0])
                layer_norm(2, g + 1)
                shared_norm(0, g)
                residual(3, g + 1, psU[1])
                low_x(1, g + 1, psY[1])
                layer_norm(3, g + 1)
                low_x(2, g + 1, psY[0])
                expert_rows(3, g)
                low_x(3, g + 1, psY[1])
                shared_sum(2, g)
                shared_sum(3, g)
                largest_logits(g + 1)
                shared_stats(2, g)
                shared_stats(3, g)
                shared_norm(1, g)
                routing(g + 1)
            for i in range(IC):
                low_square(i, GROUPS - 1)
                if i < TILES:
                    expert_rows(i, GROUPS - 1, psT)
            for j in range(TILES):
                last_rows(j, GROUPS - 1)
                if j >= 2:
                    last_scaled(j)
                if j == 3:
                    last_sum(2, GROUPS - 1)
                    last_sum(3, GROUPS - 1)

        @block.tensor
        def _(pe):
            mm = nc.tensor.matmul

            def split_product(dst, stat_hl, mov_hl, n, steps, start=True, stop=True):
                for k in range(steps):
                    for a, b in ((0, 0), (0, 1), (1, 0)):
                        last = mm(dst, stat_hl(a, k), mov_hl(b, k), start=start and k == 0 and a == b,
                                  stop=stop and k == steps - 1 and a == 1)
                return last

            def counts(b, dst):
                before = [ohr[:, i, :] for i in range(4)] if b == 1 else [] if b == 0 else [
                    ohr_sum[:, b - 2, i * P:(i + 1) * P] for i in range(4)]
                for j in range(4):
                    c = slice(j * P, (j + 1) * P)
                    earlier = before + [ohr[:, 4 * b + i, :] for i in range(j)]
                    for n, rows in enumerate(earlier):
                        mm(dst[:, c], ones[:, :], rows, start=n == 0, stop=False)
                    last = mm(dst[:, c], tri[:, :], ohr[:, 4 * b + j, :], start=not earlier, stop=True)
                last.then_inc(s_cnt, 1)

            def token_columns(n):
                pe.wait_ge(s_row, n + 1)
                for k in range(KC):
                    last = nc.tensor.transpose(psS[:, k * P:(k + 1) * P], row[:, k * P:(k + 1) * P], ident[:, :])
                last.then_inc(s_rowT, 1)

            def keep_busy(ps, n):
                for i in range(n):
                    mm(ps[:, 0:P], ident[:, :], ident[:, :], start=True, stop=True)

            pe.wait_ge(s_pool0, 10)
            keep_busy(psT, WARM_UP)
            token_columns(0)
            pe.wait_ge(ld["proj"], 16)
            pe.wait_ge(s_colT, 1)
            for k in range(KC):
                last = mm(psT[:, :], colT[:, k], pj_sb[:, k], start=k == 0, stop=k == KC - 1)
            last.then_inc(s_proj, 1)
            pe.wait_ge(s_ohr, 1)
            counts(0, bank[0])
            counts(1, bank[1])
            for j in range(SEQ // P):
                c = slice((j % 8) * P, (j % 8 + 1) * P)
                last = nc.tensor.transpose(psU[j // 8][:, :].bitcast(F16)[:, c], ohr[:, j, :], identh)
                if j % 8 == 7:
                    last.then_inc(s_ohT, 1)
            pe.wait_ge(s_tsum, 1)
            counts(2, count_bank[2])
            token_columns(1)
            pe.wait_ge(s_colT, 2)
            pe.wait_ge(s_oht, 2)
            for i, w in enumerate((wq_sb, wk_sb)):
                pe.wait_ge(ld["wq" if i == 0 else "wk"], 16)
                for m in range(KC):
                    for k in range(KC):
                        last = mm(psU[i][:, m * P:(m + 1) * P], w[:, k, m * P:(m + 1) * P], colT[:, k],
                                  start=k == 0, stop=k == KC - 1)
                last.then_inc(s_qkv, 1)
            pe.wait_ge(s_tsum, 2)
            counts(3, count_bank[3])
            pe.wait_ge(s_qk, 2)
            pe.wait_ge(s_lnraw, 3)
            for c in range(KC):
                for j in range(4):
                    r = slice(HD * j, HD * (j + 1))
                    last = mm(bank[j][:, c * P:(c + 1) * P], qT[r, c, :], kT[r, c, :], start=True, stop=True)
            last.then_inc(s_tab, 1)
            pe.wait_ge(ld["wv"], 16)
            for k in range(KC):
                last = mm(psT[:, :], colT[:, k], wv_sb[:, k], start=k == 0, stop=k == KC - 1)
            last.then_inc(s_qkv, 1)

            def table_rows(ps, t, q):
                for a in range(2):
                    last = mm(ps[:, :], oht[:, t], sc_hl[:, a, 4 * q:4 * q + 4, :].rearrange("p h v -> p (h v)"),
                              start=a == 0, stop=a == 1)
                last.then_inc(s_scored, 1)

            def score(u, g):
                q, j = u // TILES, u % TILES
                need(pe, s_added, g * UNITS + u)
                if u == 0:
                    need(pe, s_tokr, g * TILES)
                table_rows(psS, bass.ds(g * GT + j * P, P), q)

            def score_alone(u):
                j, q = u // HQ, u % HQ
                need(pe, s_added, u - 1)
                table_rows(psY[u % 2], slice(j * P, (j + 1) * P), q)

            def probs_transposed(ps, u):
                for h in range(4):
                    last = nc.tensor.transpose(ps[:, h * P:(h + 1) * P], prob[:, u % UBUF, h, :], ident[:, :])
                last.then_inc(s_trn, 1)

            def transpose_probs(u, g):
                pe.wait_ge(s_norm, g * UNITS + u + 1)
                need(pe, s_pt, g * UNITS + u)
                if u % TILES == 0 and u > 0:
                    pe.wait_ge(s_yl, g * HQ + u // TILES)
                if u == 0:
                    need(pe, s_h1, g * TILES)
                probs_transposed(psT, u)

            def transpose_probs_alone(u):
                pe.wait_ge(s_norm, u + 1)
                if u < UNITS - 1:
                    need(pe, s_pt, u)
                else:
                    pe.wait_ge(s_xl, TILES - 2)
                probs_transposed(alone_bank(u), u)

            def attend(q, g):
                pe.wait_ge(s_pt, g * UNITS + (q + 1) * TILES)
                for h in range(4):
                    c = (4 * q + h) * HD
                    last = mm(psT[HD * h:HD * (h + 1), :], val[:, c:c + HD], probT[:, q % 2, h, :],
                              start=True, stop=True)
                last.then_inc(s_pv, 1)

            def attend_alone(u):
                j, q = u // HQ, u % HQ
                pe.wait_ge(s_pt, u + 1)
                if q == 0:
                    need(pe, s_yl, j - 1)
                for h in range(4):
                    c = (4 * q + h) * HD
                    last = mm((psT, psY[3])[j % 2][HD * h:HD * (h + 1), q * P:(q + 1) * P], val[:, c:c + HD],
                              probT0[:, u % UBUF, h, :], start=True, stop=True)
                if q == HQ - 1:
                    last.then_inc(s_pv, 1)

            def token_rows(j, g):
                t = bass.ds(g * GT + j * P, P)
                for a in range(2):
                    last = mm(psS[:, :], oht[:, t], tk_hl[:, a], start=a == 0, stop=a == 1)
                last.then_inc(s_tg, 1)

            def output_rows(j, ps, chunks):
                c = slice(j * P, (j + 1) * P)
                last = split_product(ps[:, :], lambda a, k: yt_hl[:, a, chunks[k], c], lambda b, k: wo_hl[:, b, chunks[k]],
                                     DM, len(chunks), start=chunks[0] == 0, stop=chunks[-1] == KC - 1)
                if chunks[-1] == KC - 1:
                    last.then_inc(s_wo, 1)

            def attention_out(j, g):
                if j == 0:
                    pe.wait_ge(s_yl, (g + 1) * HQ)
                    pe.wait_ge(s_added, (g + 1) * UNITS)
                else:
                    pe.wait_ge(s_tokr, g * TILES + j)
                token_rows(j, g)
                if j == 1:
                    pe.wait_ge(s_moe, (g - 1) * TILES + 2)
                if j >= 2:
                    pe.wait_ge(s_h1, g * TILES + j - 1)
                output_rows(j, (psT, psU[1])[j % 2], (0, 1, 2, 3))

            def attention_out_alone(j, ps=psY[2], chunks=(0, 1)):
                need(pe, s_tokr, j)
                token_rows(j, 0)
                if ps is psY[2]:
                    need(pe, s_h1, j)
                pe.wait_ge(s_yl, j + 1)
                output_rows(j, ps, chunks)

            def transpose_rows(j, g, ps, bank_free):
                pe.wait_ge(s_x, g * TILES + j + 1)
                need(pe, *bank_free)
                for k in range(KC):
                    last = nc.tensor.transpose(ps[:, k * P:(k + 1) * P], xrow[:, j % 2, k * P:(k + 1) * P],
                                               ident[:, :])
                last.then_inc(s_xt, 1)

            def gate_logits(g):
                pe.wait_ge(s_tokr, (g + 1) * TILES)
                for j in range(TILES):
                    pe.wait_ge(s_xl, g * TILES + j + 1)
                    c = slice(j * P, (j + 1) * P)
                    last = split_product(psS[:, j * NEXP:(j + 1) * NEXP], lambda a, k: xt_hl[:, a, k, c],
                                         lambda b, k: gt_hl[:, b, k, :], NEXP, KC)
                last.then_inc(s_gate, 1)

            def up_chunk(i, g):
                if i >= 2:
                    pe.wait_ge(s_relu, g * IC + i - 1)
                c = slice(i * P, (i + 1) * P)
                split_product(psU[i % 2][:, :], lambda a, k: up_hl[:, a, k, c], lambda b, k: xt_hl[:, b, k, :], GT,
                              KC).then_inc(s_up, 1)

            def down_tile(j, i, g):
                c = slice(j * P, (j + 1) * P)
                return split_product(psY[j][:, :], lambda a, k: sq_hl[:, i % RING, a, c],
                                     lambda b, k: dn_hl[:, b, i], DM, 1, start=i == 0, stop=i == IC - 1)

            def down_chunk(i, g):
                pe.wait_ge(s_sl, g * IC + i + 1)
                for j in range(TILES):
                    last = down_tile(j, i, g)
                last.then_inc(s_dn, 1)

            def expert_product(j, g, ps=None):
                if ps is not None:
                    pe.wait_ge(s_moe, g * TILES + j)
                elif j < 2:
                    pe.wait_ge(s_relu, g * IC + IC - 1 + j)
                else:
                    pe.wait_ge(s_moe, g * TILES + 2 * j - 3)
                c = slice(j * P, (j + 1) * P)
                split_product((ps or psU[EXPERT_BANK[j]])[:, :], lambda a, k: xt_hl[:, a, k, c], lambda b, k: ex_hl[:, b, k], DM,
                              KC).then_inc(s_ex, 1)

            def gram(ps, raw, rows):
                for c in range(KC):
                    last = gram_block(ps, raw, rows, c)
                last.then_inc(s_gram, 1)

            def gram_block(ps, raw, rows, c):
                for k in range(rows):
                    w = raw[:, k * DM + c * P:k * DM + (c + 1) * P].bitcast(BF16).rearrange(
                        "p (v two) -> p v two", two=2)[:, :, 1]
                    last = mm(ps[:, c * P:(c + 1) * P], w, w, start=k == 0, stop=k == rows - 1)
                return last

            pe.wait_ge(ld["wo"], 16)
            pe.wait_ge(s_qk, 2)
            gram(psU[0], raww.rearrange("p k n -> p (k n)"), KC)
            pe.wait_ge(ld["ex"], 16)
            pe.wait_ge(s_lnraw, GROUPS)
            gram(psS, rawe.rearrange("p k n -> p (k n)"), KC)
            pe.wait_ge(s_lo, 4)
            for u in range(4):
                score_alone(u)
            for u in range(UNITS):
                transpose_probs_alone(u)
                if u == VAL_UNIT:
                    pe.wait_ge(s_val, 1)
                    for v in range(u):
                        attend_alone(v)
                elif u > VAL_UNIT:
                    attend_alone(u - 1)
                if u < UNITS - 4:
                    score_alone(u + 4)
                if u == 1:
                    pe.wait_ge(ld["dn"], 16)
                    pe.wait_ge(s_ssw, 1)
                if u in (1, 2, 3, 4):
                    last = gram_block(psU[0], rawd, IC, u - 1)
                if u == 4:
                    last.then_inc(s_gram, 1)
                j, step = u // HQ - 1, u % HQ
                if step == 0 and j >= 1:
                    transpose_rows(j - 1, 0, psU[0], (s_xl, j - 1))
                if step == 1 and 0 <= j < TILES - 2:
                    if j == 0:
                        pe.wait_ge(s_wlo, 1)
                        pe.wait_ge(s_lo, 5)
                    attention_out_alone(j)
                if step == 2 and 0 <= j < TILES - 2:
                    output_rows(j, psY[2], (2, 3))
                if u == UNITS - 3:
                    attention_out_alone(TILES - 2, chunks=(0,))
                if u == UNITS - 2:
                    output_rows(TILES - 2, psY[2], (1,))
                if u == UNITS - 1:
                    output_rows(TILES - 2, psY[2], (2,))
            attend_alone(UNITS - 1)
            output_rows(TILES - 2, psY[2], (3,))
            pe.wait_ge(s_added, UNITS)
            attention_out_alone(TILES - 1, psY[0])
            output_rows(TILES - 1, psY[0], (2, 3))
            transpose_rows(TILES - 2, 0, psU[0], (s_pt, UNITS))
            keep_busy(psU[1], KEEP_BUSY)
            transpose_rows(TILES - 1, 0, psU[0], (s_xl, TILES - 1))
            pe.wait_ge(s_wlo, 2)
            pe.wait_ge(s_uplo, KC)
            pe.wait_ge(s_dnlo, 4)
            with pe.Fori(0, GROUPS - 1) as g:
                gate_logits(g)
                for i in range(IC):
                    up_chunk(i, g)
                    if i > TILES and i % TILES == 1:
                        attend(i // TILES - 1, g + 1)
                    if i == 0:
                        pe.wait_ge(s_top, g + 1)
                    score(i, g + 1)
                    if i > 0:
                        down_chunk(i - 1, g)
                        transpose_probs(i - 1, g + 1)
                pe.wait_ge(s_exsc, 2)
                expert_product(0, g)
                transpose_probs(UNITS - 1, g + 1)
                expert_product(1, g)
                attend(HQ - 1, g + 1)
                expert_product(2, g)
                attention_out(0, g + 1)
                pe.wait_ge(s_sl, g * IC + IC)
                down_tile(0, IC - 1, g).then_inc(s_dt, 1)
                attention_out(1, g + 1)
                down_tile(1, IC - 1, g).then_inc(s_dt, 1)
                attention_out(2, g + 1)
                transpose_rows(0, g + 1, psY[0], (s_yev, g * TILES + 1))
                down_tile(2, IC - 1, g).then_inc(s_dt, 1)
                attention_out(3, g + 1)
                transpose_rows(1, g + 1, psY[1], (s_yev, g * TILES + 2))
                transpose_rows(2, g + 1, psY[0], (s_xl, g * TILES + TILES + 1))
                expert_product(3, g)
                transpose_rows(3, g + 1, psY[1], (s_xl, g * TILES + TILES + 2))
                down_tile(3, IC - 1, g).then_inc(s_dt, 1)
                pe.wait_ge(s_moe, g * TILES + 4)
            gate_logits(GROUPS - 1)
            for i in range(IC):
                up_chunk(i, GROUPS - 1)
                if i == 0:
                    pe.wait_ge(s_top, GROUPS)
                if i > 0:
                    down_chunk(i - 1, GROUPS - 1)
                if i < TILES:
                    expert_product(i, GROUPS - 1, psT)
            pe.wait_ge(s_sl, GROUPS * IC)
            for j in range(TILES):
                down_tile(j, IC - 1, GROUPS - 1).then_inc(s_dt, 1)


def kernel(x, L0_tok_emb_table, L0_tok_norm_weight, L0_tok_proj_weight, L0_attn_Wq, L0_attn_bq, L0_attn_Wk,
           L0_attn_bk, L0_attn_Wv, L0_attn_bv, L0_attn_Wo, L0_attn_bo, L0_ffn_gate_w, L0_ffn_up_w, L0_ffn_down_w,
           L0_ffn_expert_weight, L0_ffn_ln_gamma, L0_ffn_ln_beta):
    import numpy as np
    import concourse.bacc as bacc
    from concourse.bass_utils import run_bass_kernel_spmd

    def heads_last(w):
        return np.asarray(w).transpose(1, 0, 2).reshape(DM, DM)

    def column(b):
        return np.asarray(b).reshape(KC, P).T

    given = {
        "ids_col": np.asarray(x).reshape(SEQ // P, P).T, "emb": L0_tok_emb_table, "norm_w": L0_tok_norm_weight,
        "proj_t": np.asarray(L0_tok_proj_weight).T, "wq": heads_last(L0_attn_Wq), "wk": heads_last(L0_attn_Wk),
        "wv": heads_last(L0_attn_Wv), "bq": column(L0_attn_bq), "bk": column(L0_attn_bk),
        "bv": np.asarray(L0_attn_bv).reshape(DM), "wo": L0_attn_Wo, "bo": L0_attn_bo, "up": L0_ffn_up_w,
        "down": L0_ffn_down_w, "expert": L0_ffn_expert_weight, "gate": L0_ffn_gate_w, "gamma": L0_ffn_ln_gamma,
        "beta": L0_ffn_ln_beta,
    }
    nc = bacc.Bacc("TRN2", target_bir_lowering=False, num_devices=1)
    arrays, aps = {}, {}
    for name, a in given.items():
        a = np.ascontiguousarray(a)
        arrays[f"in_{name}"] = a
        aps[name] = nc.dram_tensor(f"in_{name}", a.shape, mybir.dt.from_np(a.dtype), kind="ExternalInput").ap()
    out = nc.dram_tensor("out_rows", (SEQ, DM), F32, kind="ExternalOutput").ap()
    tower(nc, out=out, **aps)
    got = run_bass_kernel_spmd(nc, [arrays], core_ids=[0]).results[0]["out_rows"]
    return got.reshape(1, SEQ, DM)
```
